# Optimizing a Trainium2 kernel written in Bass

```python
import numpy as np
import jax
import jax.numpy as jnp

def _softmax(x, axis=-1):
    return jax.nn.softmax(x, axis=axis)

def _gelu(x):
    return jax.nn.gelu(x, approximate=True)

def _silu(x):
    return jax.nn.silu(x)

def _sigmoid(x):
    return jax.nn.sigmoid(x)

def _layernorm(x, axis=-1, eps=1e-05):
    m = jnp.mean(x, axis=axis, keepdims=True)
    v = jnp.var(x, axis=axis, keepdims=True)
    return (x - m) / jnp.sqrt(v + eps)

def _scatter_add(tgt, idx, src, axis=0):
    return tgt.at[idx].add(src)

def _segment_sum(src, seg, n):
    return jax.ops.segment_sum(src, seg, n)
kernel_name = 'mk_sandwich_d1_jaxref_r8_7ac624'

def setup_inputs(seed: int=0):
    np.random.seed(seed)
    _w = jnp.asarray

    def _L0_attn_setup():
        import jax, jax.numpy as jnp
        import numpy as np
        B, S, HID = (1, 256, 512)
        H, HK, D = (32, 8, 128)
        L = D // 4
        key = jax.random.key(seed)
        ks = jax.random.split(key, 7)
        s = 0.02
        return {'hidden_states': jax.random.normal(ks[0], (B, S, HID), jnp.float32), 'Wq': jax.random.normal(ks[1], (H * D, HID), jnp.float32) * s, 'Wk_down': jax.random.normal(ks[2], (HK * L, HID), jnp.float32) * s, 'Wv_down': jax.random.normal(ks[3], (HK * L, HID), jnp.float32) * s, 'Wk_up': jax.random.normal(ks[4], (HK * D, HK * L), jnp.float32) * s, 'Wv_up': jax.random.normal(ks[5], (HK * D, HK * L), jnp.float32) * s, 'Wo': jax.random.normal(ks[6], (HID, H * D), jnp.float32) * s}
    _L0_attn_in = _L0_attn_setup()

    def _L0_ffn_setup():
        import jax, jax.numpy as jnp
        import numpy as np
        HIDDEN = 512
        MOE_INTER = 128
        SHARED_INTER = 512
        NUM_EXPERTS = 16
        TOP_K = 2

        def _moe_forward(x, gate_w, w_gate_up, w_down, shared_w_gate_up, shared_w_down):
            orig_shape = x.shape
            x2 = x.reshape(-1, orig_shape[-1])
            gu_s = x2 @ shared_w_gate_up.T
            g_s, u_s = jnp.split(gu_s, 2, axis=-1)
            shared_out = jax.nn.silu(g_s) * u_s @ shared_w_down.T
            logits = x2 @ gate_w.T
            probs = jax.nn.softmax(logits, axis=-1)
            topk_vals, topk_idx = jax.lax.top_k(probs, TOP_K)
            topk_vals = topk_vals / jnp.sum(topk_vals, axis=-1, keepdims=True)
            combine = jnp.sum(jax.nn.one_hot(topk_idx, NUM_EXPERTS, dtype=x2.dtype) * topk_vals[..., None], axis=1)
            gu = jnp.einsum('th,eih->eti', x2, w_gate_up)
            g, u = jnp.split(gu, 2, axis=-1)
            act = jax.nn.silu(g) * u
            out_e = jnp.einsum('eti,ehi->eth', act, w_down)
            moe_out = jnp.einsum('eth,te->th', out_e, combine)
            return (moe_out + shared_out).reshape(orig_shape)
        key = jax.random.key(seed)
        ks = jax.random.split(key, 6)
        s = 0.02
        hidden_states = jax.random.normal(ks[0], (2, 256, HIDDEN), dtype=jnp.float32)
        gate_w = jax.random.normal(ks[1], (NUM_EXPERTS, HIDDEN), dtype=jnp.float32) * s
        w_gate_up = jax.random.normal(ks[2], (NUM_EXPERTS, 2 * MOE_INTER, HIDDEN), dtype=jnp.float32) * s
        w_down = jax.random.normal(ks[3], (NUM_EXPERTS, HIDDEN, MOE_INTER), dtype=jnp.float32) * s
        shared_w_gate_up = jax.random.normal(ks[4], (2 * SHARED_INTER, HIDDEN), dtype=jnp.float32) * s
        shared_w_down = jax.random.normal(ks[5], (HIDDEN, SHARED_INTER), dtype=jnp.float32) * s
        return {'hidden_states': hidden_states, 'gate_w': gate_w, 'w_gate_up': w_gate_up, 'w_down': w_down, 'shared_w_gate_up': shared_w_gate_up, 'shared_w_down': shared_w_down}
    _L0_ffn_in = _L0_ffn_setup()
    _d = {'L0_attn_hidden_states': _L0_attn_in['hidden_states'], 'L0_attn_Wq': _L0_attn_in['Wq'], 'L0_attn_Wk_down': _L0_attn_in['Wk_down'], 'L0_attn_Wv_down': _L0_attn_in['Wv_down'], 'L0_attn_Wk_up': _L0_attn_in['Wk_up'], 'L0_attn_Wv_up': _L0_attn_in['Wv_up'], 'L0_attn_Wo': _L0_attn_in['Wo'], 'L0_ffn_gate_w': _L0_ffn_in['gate_w'], 'L0_ffn_w_gate_up': _L0_ffn_in['w_gate_up'], 'L0_ffn_w_down': _L0_ffn_in['w_down'], 'L0_ffn_shared_w_gate_up': _L0_ffn_in['shared_w_gate_up'], 'L0_ffn_shared_w_down': _L0_ffn_in['shared_w_down']}
    _x0 = _d['L0_attn_hidden_states']
    _d['L0_attn_hidden_states'] = jax.random.normal(jax.random.fold_in(jax.random.key(seed), 1), (4, 256, 512), dtype=_x0.dtype)
    del _x0
    return _d

def reference(L0_attn_hidden_states, L0_attn_Wq, L0_attn_Wk_down, L0_attn_Wv_down, L0_attn_Wk_up, L0_attn_Wv_up, L0_attn_Wo, L0_ffn_gate_w, L0_ffn_w_gate_up, L0_ffn_w_down, L0_ffn_shared_w_gate_up, L0_ffn_shared_w_down):

    def _L0_attn_ref(hidden_states, Wq, Wk_down, Wv_down, Wk_up, Wv_up, Wo):
        import jax, jax.numpy as jnp
        import numpy as np
        B, S, HID = (1, 256, 512)
        H, HK, D = (32, 8, 128)
        L = D // 4
        b, s, _ = hidden_states.shape
        q = (hidden_states @ Wq.T).reshape(b, s, H, D).transpose(0, 2, 1, 3)
        kc = (hidden_states @ Wk_down.T).reshape(b, s, HK, L).transpose(0, 2, 1, 3)
        vc = (hidden_states @ Wv_down.T).reshape(b, s, HK, L).transpose(0, 2, 1, 3)
        lat = jnp.concatenate([kc, vc], axis=-1).reshape(b, s, HK * 2 * L)
        k_cmp, v_cmp = jnp.split(lat, 2, axis=-1)
        k = (k_cmp @ Wk_up.T).reshape(b, s, HK, D).transpose(0, 2, 1, 3)
        v = (v_cmp @ Wv_up.T).reshape(b, s, HK, D).transpose(0, 2, 1, 3)
        n_rep = H // HK
        k = jnp.repeat(k, n_rep, axis=1)
        v = jnp.repeat(v, n_rep, axis=1)
        scale = 1.0 / jnp.sqrt(jnp.asarray(D, hidden_states.dtype))
        scores = jnp.einsum('bhqd,bhkd->bhqk', q, k) * scale
        causal = jnp.tril(jnp.ones((s, s), dtype=bool))
        scores = jnp.where(causal, scores, jnp.asarray(-1000000000.0, scores.dtype))
        attn = jax.nn.softmax(scores, axis=-1)
        out = jnp.einsum('bhqk,bhkd->bhqd', attn, v)
        out = out.transpose(0, 2, 1, 3).reshape(b, s, H * D)
        return out @ Wo.T

    def _L0_ffn_ref(hidden_states, gate_w, w_gate_up, w_down, shared_w_gate_up, shared_w_down):
        import jax, jax.numpy as jnp
        import numpy as np
        HIDDEN = 512
        MOE_INTER = 128
        SHARED_INTER = 512
        NUM_EXPERTS = 16
        TOP_K = 2

        def _moe_forward(x, gate_w, w_gate_up, w_down, shared_w_gate_up, shared_w_down):
            orig_shape = x.shape
            x2 = x.reshape(-1, orig_shape[-1])
            gu_s = x2 @ shared_w_gate_up.T
            g_s, u_s = jnp.split(gu_s, 2, axis=-1)
            shared_out = jax.nn.silu(g_s) * u_s @ shared_w_down.T
            logits = x2 @ gate_w.T
            probs = jax.nn.softmax(logits, axis=-1)
            topk_vals, topk_idx = jax.lax.top_k(probs, TOP_K)
            topk_vals = topk_vals / jnp.sum(topk_vals, axis=-1, keepdims=True)
            combine = jnp.sum(jax.nn.one_hot(topk_idx, NUM_EXPERTS, dtype=x2.dtype) * topk_vals[..., None], axis=1)
            gu = jnp.einsum('th,eih->eti', x2, w_gate_up)
            g, u = jnp.split(gu, 2, axis=-1)
            act = jax.nn.silu(g) * u
            out_e = jnp.einsum('eti,ehi->eth', act, w_down)
            moe_out = jnp.einsum('eth,te->th', out_e, combine)
            return (moe_out + shared_out).reshape(orig_shape)
        return _moe_forward(hidden_states, gate_w, w_gate_up, w_down, shared_w_gate_up, shared_w_down)
    x = L0_attn_hidden_states
    x = x + _layernorm(_L0_attn_ref(_layernorm(x, axis=-1), L0_attn_Wq, L0_attn_Wk_down, L0_attn_Wv_down, L0_attn_Wk_up, L0_attn_Wv_up, L0_attn_Wo), axis=-1)
    x = x + _layernorm(_L0_ffn_ref(_layernorm(x, axis=-1), L0_ffn_gate_w, L0_ffn_w_gate_up, L0_ffn_w_down, L0_ffn_shared_w_gate_up, L0_ffn_shared_w_down), axis=-1)
    return x

_drawn_inputs = setup_inputs


def setup_inputs(seed=0):
    import zlib

    import numpy as np

    out = dict(_drawn_inputs(seed))
    spreads = {}
    factors = {}
    for name, (base, spread) in spreads.items():
        noise = np.random.default_rng([zlib.crc32(name.encode()), seed]).standard_normal(out[name].shape)
        drawn = base * np.exp(spread * noise) if base else spread * noise
        out[name] = jnp.asarray(drawn.astype(out[name].dtype))
    for name, factor in factors.items():
        out[name] = (out[name] * factor).astype(out[name].dtype)
    return out
```

```python
from contextlib import ExitStack

import concourse.bass as bass
from concourse import mybir

ALU = mybir.AluOpType
ACT = mybir.ActivationFunctionType
AX_X = mybir.AxisListType.X
F32 = mybir.dt.float32
F32R = mybir.dt.float32r

P = 128
EPS = 1e-5
MASKED = -1e30

B, S, HID = 4, 256, 512
NG, HPG, D = 8, 4, 128
T = B * S
TILES = T // P
CH = HID // P
PAIR = 2 * S
STEPS = 8
NSTEP = NG * STEPS

NE, INTER, SHARED = 16, 128, 512
NX = NE + SHARED // INTER
HALF = 512
UNITS = 2 * NX


def build_program(nc, x, w_lat, w_q, w_o, w_kv, w_gate, w_gu, w_dn, out):
    x_tiles = x.rearrange("(t p) h -> p t h", p=P)
    out_tiles = out.rearrange("(t p) h -> p t h", p=P)

    top = ExitStack()
    with top:
        def sem(name):
            return top.enter_context(nc.semaphore(name))

        def allocate(stack):
            return lambda name, shape, dt=F32: stack.enter_context(nc.sbuf_tensor(name, shape, dt))

        psS = top.enter_context(nc.psum_tensor("psS", [P, 2, 512], F32))
        psT = top.enter_context(nc.psum_tensor("psT", [P, 2, 512], F32))
        psO = top.enter_context(nc.psum_tensor("psO", [P, 512], F32))
        psQ = top.enter_context(nc.psum_tensor("psQ", [P, 512], F32))
        psW = top.enter_context(nc.psum_tensor("psW", [P, 512], F32))
        psKV = top.enter_context(nc.psum_tensor("psKV", [P, 512], F32))
        bank_gate = [psS[:, 0, :], psS[:, 1, :]]
        bank_up = [psT[:, 0, :], psT[:, 1, :]]
        bank_down = [psO[:], psQ[:], psW[:], psKV[:]]
        bank_turn = [psS[:, 0, :], psS[:, 1, :]]
        bank_lat = [psT[:, 0, :], psT[:, 1, :], psO[:]]

        sb = allocate(top)
        ident = sb("ident", [P, P])
        mask = sb("mask", [P, 2, 256])
        zero = sb("zero", [P, 1])
        waiter = sb("waiter", [P, 4])
        xT_hi = sb("xT_hi", [P, CH, T], F32R)
        xT_lo = sb("xT_lo", [P, CH, T], F32R)
        acc = sb("acc", [P, TILES, HID])
        bn = sb("bn", [P, TILES, 6])
        mean_var = sb("mean_var", [P, TILES, 2])
        veps = sb("veps", [P, TILES])
        std = sb("std", [P, TILES])
        rstd = sb("rstd", [P, TILES])
        smax = sb("smax", [P, 2, 4])
        nmax = sb("nmax", [P, 2, 4])
        rsum = sb("rsum", [P, 2, 4])
        rinv = sb("rinv", [P, 2, 4])

        attn = ExitStack()
        early = ExitStack()
        sa = allocate(early)
        x_in = sa("x_in", [P, TILES, HID])
        wl_raw = sa("wl_raw", [P, CH, HID])
        wl_hi = sa("wl_hi", [P, CH, HID], F32R)
        wl_lo = sa("wl_lo", [P, CH, HID], F32R)
        early.close()
        sa = allocate(attn)
        o_hi = sa("o_hi", [P, 2, HPG, S], F32R)
        o_lo = sa("o_lo", [P, 2, HPG, S], F32R)
        s_sb = [sa(f"s_sb{i}", [P, 2, 2, 256]) for i in range(2)]
        pT_hi = sa("pT_hi", [P, 768], F32R)
        pT_lo = sa("pT_lo", [P, 768], F32R)
        k_hi = [sa(f"k_hi{i}", [P, PAIR], F32R) for i in range(2)]
        k_lo = [sa(f"k_lo{i}", [P, PAIR], F32R) for i in range(2)]
        v_hi = [sa(f"v_hi{i}", [P, 4, D], F32R) for i in range(2)]
        v_lo = [sa(f"v_lo{i}", [P, 4, D], F32R) for i in range(2)]
        q_hi = [sa(f"q_hi{i}", [P, HPG, PAIR], F32R) for i in range(2)]
        q_lo = [sa(f"q_lo{i}", [P, HPG, PAIR], F32R) for i in range(2)]
        lat = sa("lat", [P, 4, T])
        raw = sa("raw", [P, 4, 512])
        wkv = sa("wkv", [P, 2, 2, D])
        wq_hi = sa("wq_hi", [P, HPG, CH, D], F32R)
        wq_lo = sa("wq_lo", [P, HPG, CH, D], F32R)
        wo_hi = sa("wo_hi", [P, 2, HPG, HID], F32R)
        wo_lo = sa("wo_lo", [P, 2, HPG, HID], F32R)
        attn.close()

        ffn = ExitStack()
        sf = allocate(ffn)
        x1 = sf("x1", [P, TILES, HID])
        acc2 = sf("acc2", [P, TILES, HID])
        xn = sf("xn", [P, 2, HID])
        w_g = sf("w_g", [P, CH, NE])
        probs = sf("probs", [P, TILES, NE])
        left = sf("left", [P, TILES, NE])
        first = sf("first", [P, TILES, NE])
        second = sf("second", [P, TILES, NE])
        rank = sf("rank", [P, TILES, NE])
        top1 = sf("top1", [P, TILES])
        top2 = sf("top2", [P, TILES])
        low = sf("low", [P, TILES])
        tsum = sf("tsum", [P, TILES])
        tinv = sf("tinv", [P, TILES])
        comb = sf("comb", [P, NX, TILES])
        comb_e = sf("comb_e", [P, 2, TILES])
        silu = [sf(f"silu{i}", [P, HALF]) for i in range(2)]
        hid = [sf(f"hid{i}", [P, HALF]) for i in range(2)]
        hid_hi = [sf(f"hid_hi{i}", [P, HALF], F32R) for i in range(2)]
        hid_lo = [sf(f"hid_lo{i}", [P, HALF], F32R) for i in range(2)]
        gu_raw = [sf(f"gu_raw{i}", [P, CH, 256]) for i in range(2)]
        dn_raw = [sf(f"dn_raw{i}", [P, HID]) for i in range(2)]
        gu_hi = [sf(f"gu_hi{i}", [P, CH, 256], F32R) for i in range(2)]
        gu_lo = [sf(f"gu_lo{i}", [P, CH, 256], F32R) for i in range(2)]
        dn_hi = [sf(f"dn_hi{i}", [P, HID], F32R) for i in range(2)]
        dn_lo = [sf(f"dn_lo{i}", [P, HID], F32R) for i in range(2)]
        ffn.close()

        x_in_landed = [sem(f"x_in_landed{i}") for i in range(4)]
        wl_landed = sem("wl_landed")
        raw_landed = [sem(f"raw_landed{i}") for i in range(4)]
        wkv_landed = sem("wkv_landed")
        x1_landed = sem("x1_landed")
        gate_landed = sem("gate_landed")
        gu_landed = [sem(f"gu_landed{i}") for i in range(2)]
        dn_landed = [sem(f"dn_landed{i}") for i in range(2)]
        out_stored = sem("out_stored")
        const_step = sem("const_step")
        consts_ready = sem("consts_ready")
        acc_zeroed = sem("acc_zeroed")
        acc2_zeroed = sem("acc2_zeroed")
        bn_done = sem("bn_done")
        aggr_done = sem("aggr_done")
        veps_done = sem("veps_done")
        std_done = sem("std_done")
        rstd_done = sem("rstd_done")
        xn_done = sem("xn_done")
        turn_mm = sem("turn_mm")
        xT_hi_done = sem("xT_hi_done")
        xT_lo_done = sem("xT_lo_done")
        wl_hi_done = sem("wl_hi_done")
        wl_lo_done = sem("wl_lo_done")
        lat_mm = sem("lat_mm")
        lat_even_done = sem("lat_even_done")
        lat_odd_done = sem("lat_odd_done")
        wq_hi_done = sem("wq_hi_done")
        wq_cut = sem("wq_cut")
        wo_hi_done = sem("wo_hi_done")
        wo_cut = sem("wo_cut")
        score_mm = sem("score_mm")
        score_max = sem("score_max")
        nmax_done = sem("nmax_done")
        exp_done = sem("exp_done")
        rinv_done = sem("rinv_done")
        prob_done = sem("prob_done")
        pT_mm = sem("pT_mm")
        pT_hi_done = sem("pT_hi_done")
        pT_lo_done = sem("pT_lo_done")
        o_mm = sem("o_mm")
        o_hi_done = sem("o_hi_done")
        o_lo_done = sem("o_lo_done")
        q_mm = sem("q_mm")
        q_hi_done = sem("q_hi_done")
        q_lo_done = sem("q_lo_done")
        kv_mm = sem("kv_mm")
        kv_hi_done = sem("kv_hi_done")
        kv_lo_done = sem("kv_lo_done")
        w_mm = sem("w_mm")
        w_added = sem("w_added")
        norm_step = sem("norm_step")
        router_mm = sem("router_mm")
        router_exp = sem("router_exp")
        router_step = sem("router_step")
        gu_hi_done = sem("gu_hi_done")
        gu_cut = sem("gu_cut")
        dn_hi_done = sem("dn_hi_done")
        dn_cut = sem("dn_cut")
        g_mm = sem("g_mm")
        u_mm = sem("u_mm")
        silu_done = sem("silu_done")
        hid_done = sem("hid_done")
        hid_hi_done = sem("hid_hi_done")
        hid_lo_done = sem("hid_lo_done")
        d_mm = sem("d_mm")
        d_added = sem("d_added")
        comb_e_done = sem("comb_e_done")
        y_step = sem("y_step")
        y_done = sem("y_done")

        def fp(t):
            return t.bitcast(F32)

        def wait(eng, s, value):
            if not (isinstance(value, int) and value <= 0):
                eng.wait_ge(s, value)

        def groups(eng, body):
            body(0, True, False)
            with eng.Fori(1, NG - 1) as g:
                body(g, False, False)
            body(NG - 1, False, True)


        block = top.enter_context(nc.Block())

        @block.sync
        def _(sp):
            for i in range(4):
                sp.dma_start(x_in[:, 2 * i:2 * i + 2, :], x_tiles[:, 2 * i:2 * i + 2, :]).then_inc(x_in_landed[i], 16)
                if i == 0:
                    sp.dma_start(wl_raw[:], w_lat.rearrange("p (c n) -> p c n", c=CH)).then_inc(wl_landed, 16)

            def pieces(g, first, last):
                if first:
                    sp.dma_start(wkv[:], w_kv[0].rearrange("p (a c d) -> p a c d", a=2, c=2)).then_inc(wkv_landed, 16)
                for h in range(HPG):
                    for kind, (weights, cut) in enumerate(((w_q, wq_cut), (w_o, wo_cut))):
                        slot = 2 * (h % 2) + kind
                        if not (first and h < 2):
                            wait(sp, cut, 4 * g + h - 1)
                        sp.dma_start(raw[:, slot, :], weights[HPG * g + h]).then_inc(raw_landed[slot], 16)
                if not first:
                    wait(sp, kv_mm, 4 * g)
                    sp.dma_start(wkv[:], w_kv[g].rearrange("p (a c d) -> p a c d", a=2, c=2)).then_inc(wkv_landed, 16)

            groups(sp, pieces)

            sp.wait_ge(w_mm, NSTEP)
            sp.wait_ge(o_lo_done, NSTEP)
            sp.dma_start(x1[:], x_tiles).then_inc(x1_landed, 16)
            sp.dma_start(w_g[:], w_gate.rearrange("p (c e) -> p c e", c=CH)).then_inc(gate_landed, 16)

            def expert(e, j, first):
                if not first:
                    wait(sp, gu_cut, e - 1)
                sp.dma_start(gu_raw[j][:], w_gu[e].rearrange("p (c n) -> p c n", c=CH)).then_inc(gu_landed[j], 16)
                if not first:
                    wait(sp, dn_cut, e - 1)
                sp.dma_start(dn_raw[j][:], w_dn[e]).then_inc(dn_landed[j], 16)

            expert(0, 0, True)
            expert(1, 1, True)
            with sp.Fori(1, NX // 2) as pair:
                expert(2 * pair, 0, False)
                expert(2 * pair + 1, 1, False)

            for t in range(TILES):
                sp.wait_ge(y_done, t + 1)
                sp.dma_start(out_tiles[:, t, :], acc2[:, t, :]).then_inc(out_stored, 16)
            sp.wait_ge(out_stored, 16 * TILES)

        @block.gpsimd
        def _(pool):
            nc.gpsimd.memset(ident[:], 0.0).then_inc(const_step, 1)
            nc.gpsimd.memset(mask[:], 0.0).then_inc(const_step, 1)
            nc.gpsimd.memset(zero[:], 0.0).then_inc(const_step, 1)
            pool.wait_ge(const_step, 3)
            nc.gpsimd.affine_select(out=ident[:], in_=ident[:], compare_op=ALU.not_equal, fill=1.0, base=0,
                                    pattern=[[-1, P]], channel_multiplier=1).then_inc(consts_ready, 1)
            for t in range(2):
                nc.gpsimd.affine_select(out=mask[:, t, :], in_=mask[:, t, :], compare_op=ALU.is_ge, fill=MASKED,
                                        base=P * t, pattern=[[-1, 256]], channel_multiplier=1).then_inc(consts_ready, 1)
            nc.gpsimd.memset(acc[:], 0.0).then_inc(acc_zeroed, 1)

            def round_to(dst, src):
                z = zero[:]
                for n in src.shape[2:]:
                    z = z.rearrange("p (a b) -> p a b", b=1) if len(z.shape) < len(src.shape) else z
                return nc.gpsimd.tensor_tensor(dst, src, z.to_broadcast(list(src.shape)), ALU.add)

            for c in range(CH):
                pool.wait_ge(wl_hi_done, c + 1)
                nc.gpsimd.tensor_tensor(wl_lo[:, c, :], wl_raw[:, c, :], fp(wl_hi[:, c, :]),
                                        ALU.subtract).then_inc(wl_lo_done, 1)

            def cut(g, first, last):
                for h in range(HPG):
                    if not first:
                        wait(pool, q_mm, 8 * g + h - 3)
                    wait(pool, raw_landed[2 * (h % 2)], 32 * g + 16 * (h // 2) + 16)
                    src = raw[:, 2 * (h % 2), :].rearrange("p (c d) -> p c d", c=CH)
                    round_to(wq_hi[:, h], src).then_inc(wq_hi_done, 1)
                    wait(pool, wq_hi_done, 4 * g + h + 1)
                    nc.gpsimd.tensor_tensor(wq_lo[:, h], src, fp(wq_hi[:, h]), ALU.subtract).then_inc(wq_cut, 1)
                    if first:
                        pool.wait_ge(lat_mm, 8)
                    elif h == 0:
                        wait(pool, w_mm, 8 * g - 8)
                    wait(pool, raw_landed[2 * (h % 2) + 1], 32 * g + 16 * (h // 2) + 16)
                    src = raw[:, 2 * (h % 2) + 1, :]
                    slot = g % 2
                    round_to(wo_hi[:, slot, h], src).then_inc(wo_hi_done, 1)
                    wait(pool, wo_hi_done, 4 * g + h + 1)
                    nc.gpsimd.tensor_tensor(wo_lo[:, slot, h], src, fp(wo_hi[:, slot, h]),
                                            ALU.subtract).then_inc(wo_cut, 1)

            groups(pool, cut)

            pool.wait_ge(w_mm, NSTEP)
            pool.wait_ge(o_lo_done, NSTEP)
            nc.gpsimd.memset(acc2[:], 0.0).then_inc(acc2_zeroed, 1)

            def expert(i, j, first):
                e = 2 * i + j
                wait(pool, gu_landed[j], 16 * i + 16)
                if not first:
                    wait(pool, u_mm, 2 * e - 2)
                round_to(gu_hi[j][:], gu_raw[j][:]).then_inc(gu_hi_done, 1)
                wait(pool, gu_hi_done, e + 1)
                nc.gpsimd.tensor_tensor(gu_lo[j][:], gu_raw[j][:], fp(gu_hi[j][:]), ALU.subtract).then_inc(gu_cut, 1)
                wait(pool, dn_landed[j], 16 * i + 16)
                if not first:
                    wait(pool, d_mm, 8 * e - 8)
                round_to(dn_hi[j][:], dn_raw[j][:]).then_inc(dn_hi_done, 1)
                wait(pool, dn_hi_done, e + 1)
                nc.gpsimd.tensor_tensor(dn_lo[j][:], dn_raw[j][:], fp(dn_hi[j][:]), ALU.subtract).then_inc(dn_cut, 1)

            expert(0, 0, True)
            expert(0, 1, True)
            with pool.Fori(1, NX // 2) as pair:
                expert(pair, 0, False)
                expert(pair, 1, False)

        @block.tensor
        def _(pe):
            def three(dst, hi_l, lo_l, hi_r, lo_r, start, stop):
                nc.tensor.matmul(dst, hi_l, hi_r, start=start, stop=False)
                nc.tensor.matmul(dst, hi_l, lo_r, start=False, stop=False)
                return nc.tensor.matmul(dst, lo_l, hi_r, start=False, stop=stop)

            pe.wait_ge(consts_ready, 1)
            for t in range(TILES):
                pe.wait_ge(xn_done, t + 1)
                wait(pe, xT_lo_done, t - 1)
                for c in range(CH):
                    mm = nc.tensor.transpose(bank_turn[t % 2][:, c * P:(c + 1) * P],
                                             x_in[:, t, c * P:(c + 1) * P], ident[:])
                mm.then_inc(turn_mm, 1)

            pe.wait_ge(wl_hi_done, CH)
            pe.wait_ge(wl_lo_done, CH)
            for j in range(8):
                half, hp = j // 4, j % 4
                pe.wait_ge(xT_lo_done, 4 * half + 4)
                wait(pe, lat_even_done, 2 * (j - 2))
                wait(pe, lat_odd_done, 2 * (j - 2))
                rows = slice(hp * P, (hp + 1) * P)
                cols = slice(half * PAIR, (half + 1) * PAIR)
                for c in range(CH):
                    mm = three(bank_lat[j % 3], wl_hi[:, c, rows], wl_lo[:, c, rows],
                               xT_hi[:, c, cols], xT_lo[:, c, cols], c == 0, c == CH - 1)
                mm.then_inc(lat_mm, 1)

            def keys(u, par):
                for c in range(2):
                    mm = nc.tensor.matmul(psKV[:], wkv[:, 0, c, :], lat[:, c, par * PAIR:(par + 1) * PAIR],
                                          start=c == 0, stop=c == 1)
                mm.then_inc(kv_mm, 1)

            def values(u, par):
                for t in range(4):
                    for c in range(2):
                        mm = nc.tensor.matmul(psKV[:, t * D:(t + 1) * D],
                                              lat[:, 2 + c, par * PAIR + t * P:par * PAIR + (t + 1) * P],
                                              wkv[:, 1, c, :], start=c == 0, stop=c == 1)
                mm.then_inc(kv_mm, 1)

            def queries(h, par):
                for c in range(CH):
                    mm = three(psQ[:], wq_hi[:, h, c, :], wq_lo[:, h, c, :],
                               xT_hi[:, c, par * PAIR:(par + 1) * PAIR], xT_lo[:, c, par * PAIR:(par + 1) * PAIR],
                               c == 0, c == CH - 1)
                mm.then_inc(q_mm, 1)

            def scores(n, l):
                par, b_in, hp = l // 4, l % 4 // 2, l % 2
                u_done = 4 * (n // 4) if isinstance(n, int) else n - l % 4
                wait(pe, kv_lo_done, 2 * (n // 4) + 1 if isinstance(n, int) else (n - l % 4) // 2 + 1)
                wait(pe, q_lo_done, u_done + 2 * hp + 2)
                for j in range(2):
                    h = 2 * hp + j
                    wait(pe, score_max, 4 * n - 2 + 2 * j)
                    for qt in range(2):
                        at = slice(b_in * S + qt * P, b_in * S + (qt + 1) * P)
                        ks = slice(b_in * S, (b_in + 1) * S)
                        mm = three(psS[:, j, qt * 256:(qt + 1) * 256], q_hi[par][:, h, at], q_lo[par][:, h, at],
                                   k_hi[par][:, ks], k_lo[par][:, ks], True, True)
                    mm.then_inc(score_mm, 1)

            def turn_probs(n, l):
                wait(pe, prob_done, 4 * n + 4)
                wait(pe, pT_lo_done, n)
                p_sb = s_sb[l % 2]
                for j in range(2):
                    for qt in range(2):
                        nc.tensor.transpose(psT[:, 0, j * 256 + qt * P:j * 256 + (qt + 1) * P],
                                            p_sb[:, j, qt, 0:P], ident[:])
                    mm = nc.tensor.transpose(psT[:, 1, j * P:(j + 1) * P], p_sb[:, j, 1, P:2 * P], ident[:])
                mm.then_inc(pT_mm, 1)

            def attend(n, l):
                par, b_in = l // 4, l % 4 // 2
                wait(pe, pT_lo_done, n + 1)
                if l % 4 == 0:
                    wait(pe, kv_lo_done, n // 2 + 2 if isinstance(n, int) else n // 2 + 2)
                wait(pe, o_lo_done, n)
                v0, v1 = 2 * b_in, 2 * b_in + 1
                three(psO[:], v_hi[par][:, v0, :], v_lo[par][:, v0, :], pT_hi[:, 0:512], pT_lo[:, 0:512], True, False)
                late = psO[:].rearrange("p (j q) -> p j q", j=2)[:, :, P:2 * P]
                mm = three(late, v_hi[par][:, v1, :], v_lo[par][:, v1, :],
                           pT_hi[:, 512:768].rearrange("p (j q) -> p j q", j=2),
                           pT_lo[:, 512:768].rearrange("p (j q) -> p j q", j=2), False, True)
                mm.then_inc(o_mm, 1)

            def project(m, lm, slot):
                b_in, tt = lm % 4 // 2, lm % 2
                wait(pe, o_lo_done, m - tt + 2)
                wait(pe, w_added, m)
                for h in range(HPG):
                    at = slice(tt * P, (tt + 1) * P)
                    mm = three(psW[:], o_hi[:, b_in, h, at], o_lo[:, b_in, h, at],
                               wo_hi[:, slot, h, :], wo_lo[:, slot, h, :], h == 0, h == HPG - 1)
                mm.then_inc(w_mm, 1)

            pe.wait_ge(wkv_landed, 16)
            pe.wait_ge(lat_even_done, 16)
            pe.wait_ge(lat_odd_done, 16)
            keys(0, 0)
            for h in range(HPG):
                pe.wait_ge(wq_cut, h + 1)
                wait(pe, q_lo_done, h)
                queries(h, 0)
                if h == 1:
                    pe.wait_ge(kv_lo_done, 1)
                    values(0, 0)
            scores(0, 0)

            def steps(g, first, last):
                for l in range(STEPS):
                    n = STEPS * g + l
                    par, s = l // 4, l % 4
                    if not (last and l == STEPS - 1):
                        scores(n + 1, (l + 1) % STEPS)
                    if not (last and par == 1):
                        wait(pe, wq_cut, 4 * g + s + 1 + 4 * par)
                        wait(pe, q_lo_done, n + 4)
                        queries(s, 1 - par)
                        if s < 2:
                            if s == 0 and par == 1:
                                wait(pe, wkv_landed, 16 * g + 32)
                            wait(pe, kv_lo_done, (4 * g + 2 * par + 2) + s)
                            (keys if s == 0 else values)(None, 1 - par)
                    turn_probs(n, l)
                    if not (first and l < 2):
                        lm = (l - 2) % STEPS
                        if l == 2:
                            wait(pe, wo_cut, 4 * g + 4)
                        project(n - 2, lm, (g if l >= 2 else g + 1) % 2)
                    attend(n, l)

            groups(pe, steps)
            project(NSTEP - 2, 6, (NG - 1) % 2)
            project(NSTEP - 1, 7, (NG - 1) % 2)

            pe.wait_ge(gate_landed, 16)
            for t in range(TILES):
                pe.wait_ge(xn_done, TILES + t + 1)
                wait(pe, xT_lo_done, TILES + t - 1)
                for c in range(CH):
                    mm = nc.tensor.transpose(bank_turn[t % 2][:, c * P:(c + 1) * P],
                                             xn[:, t % 2, c * P:(c + 1) * P], ident[:])
                mm.then_inc(turn_mm, 1)
                if t >= 1:
                    logits = psT[:, 0, (t - 1) * NE:t * NE]
                    pe.wait_ge(xT_lo_done, TILES + t)
                    for c in range(CH):
                        for part, x_part in enumerate((xT_hi, xT_lo)):
                            nc.tensor.matmul(logits, fp(x_part[:, c, (t - 1) * P:t * P]), w_g[:, c, :],
                                             start=c == 0 and part == 0, stop=c == CH - 1 and part == 1)
            t = TILES
            logits = psT[:, 0, (t - 1) * NE:t * NE]
            pe.wait_ge(xT_lo_done, TILES + t)
            for c in range(CH):
                for part, x_part in enumerate((xT_hi, xT_lo)):
                    mm = nc.tensor.matmul(logits, fp(x_part[:, c, (t - 1) * P:t * P]), w_g[:, c, :],
                                          start=c == 0 and part == 0, stop=c == CH - 1 and part == 1)
            mm.then_inc(router_mm, 1)

            def gate_up(w, e, th, j, first):
                if th == 0:
                    wait(pe, gu_cut, e + 1)
                if not first:
                    wait(pe, silu_done, w - 1)
                elif w == 0:
                    pe.wait_ge(router_exp, 1)
                cols = slice(th * HALF, (th + 1) * HALF)
                for c in range(CH):
                    mm = three(bank_gate[th], gu_hi[j][:, c, 0:P], gu_lo[j][:, c, 0:P],
                               xT_hi[:, c, cols], xT_lo[:, c, cols], c == 0, c == CH - 1)
                mm.then_inc(g_mm, 1)
                if not first:
                    wait(pe, hid_done, w - 1)
                for c in range(CH):
                    mm = three(bank_up[th], gu_hi[j][:, c, P:2 * P], gu_lo[j][:, c, P:2 * P],
                               xT_hi[:, c, cols], xT_lo[:, c, cols], c == 0, c == CH - 1)
                mm.then_inc(u_mm, 1)

            def down(w, e, th, j, first):
                wait(pe, hid_lo_done, w + 1)
                if th == 0:
                    wait(pe, dn_cut, e + 1)
                for i in range(4):
                    if not first:
                        wait(pe, d_added, 4 * w + i - 3)
                    at = slice(i * P, (i + 1) * P)
                    three(bank_down[i], hid_hi[th][:, at], hid_lo[th][:, at], dn_hi[j][:], dn_lo[j][:],
                          True, True).then_inc(d_mm, 1)

            def pair_units(i, first):
                for j in range(2):
                    for th in range(2):
                        w = 4 * i + 2 * j + th
                        gate_up(w, 2 * i + j, th, j, first and j == 0)
                        if not (first and j == 0 and th == 0):
                            pj, pth = (j, 0) if th == 1 else (1 - j, 1)
                            down(w - 1, 2 * i + j - (1 - th), pth, pj, first and j == 0)

            pair_units(0, True)
            with pe.Fori(1, NX // 2) as i:
                pair_units(i, False)
            down(UNITS - 1, NX - 1, 1, 1, False)

        @block.vector
        def _(dve):
            def stats(src, t, count):
                nc.vector.bn_stats(bn[:, t, :], src).then_inc(bn_done, 1)
                dve.wait_ge(bn_done, count)
                nc.vector.bn_aggr(mean_var[:, t, :], bn[:, t, :]).then_inc(aggr_done, 1)

            def add_eps(t0, t1, aggr, count):
                dve.wait_ge(aggr_done, aggr)
                nc.vector.tensor_scalar(veps[:, t0:t1], mean_var[:, t0:t1, 1], EPS, None, ALU.add).then_inc(veps_done, 1)

            def invert(t0, t1, count):
                dve.wait_ge(std_done, count)
                nc.vector.reciprocal(rstd[:, t0:t1], std[:, t0:t1]).then_inc(rstd_done, 1)
                dve.wait_ge(rstd_done, count)

            def normalise(dst, src, t):
                return nc.vector.tensor_scalar(dst, src, mean_var[:, t, 0:1], rstd[:, t:t + 1],
                                               ALU.subtract, ALU.mult)

            for half in range(2):
                for t in range(4 * half, 4 * half + 4):
                    dve.wait_ge(x_in_landed[t // 2], 16)
                    stats(x_in[:, t, :], t, t + 1)
                add_eps(4 * half, 4 * half + 4, 4 * half + 4, half + 1)
                invert(4 * half, 4 * half + 4, half + 1)
                for t in range(4 * half, 4 * half + 4):
                    normalise(x_in[:, t, :], x_in[:, t, :], t).then_inc(xn_done, 1)

            def turned(t, count):
                dve.wait_ge(xT_hi_done, count)
                nc.vector.tensor_tensor(xT_lo[:, :, t * P:(t + 1) * P],
                                        bank_turn[t % 2].rearrange("p (c q) -> p c q", c=CH),
                                        fp(xT_hi[:, :, t * P:(t + 1) * P]), ALU.subtract).then_inc(xT_lo_done, 1)

            for t in range(TILES):
                turned(t, t + 1)

            def latents(j, e, copy):
                half, hp = j // 4, j % 4
                src = bank_lat[j % 3][64 * e:64 * e + 64, :].rearrange("p (b t c r) -> p r c b t", b=2, t=32, c=4)
                for r in range(2):
                    dst = lat[64 * r:64 * r + 64, :, half * PAIR:(half + 1) * PAIR].rearrange(
                        "p c (b t) -> p c b t", b=2)[:, :, :, (2 * hp + e) * 32:(2 * hp + e) * 32 + 32]
                    copy(dst, src[:, r])

            for j in range(8):
                dve.wait_ge(lat_mm, j + 1)
                latents(j, 1, lambda d, s: nc.vector.tensor_copy(d, s).then_inc(lat_odd_done, 1))

            def kv_low(count, dst_hi, dst_lo):
                wait(dve, kv_hi_done, count)
                nc.vector.tensor_tensor(dst_lo, psKV[:], fp(dst_hi), ALU.subtract).then_inc(kv_lo_done, 1)

            def q_low(count, par, h):
                wait(dve, q_hi_done, count)
                nc.vector.tensor_tensor(q_lo[par][:, h, :], psQ[:], fp(q_hi[par][:, h, :]),
                                        ALU.subtract).then_inc(q_lo_done, 1)

            def row_max(n, l):
                for j in range(2):
                    wait(dve, score_mm, 2 * n + j + 1)
                    if j == 0:
                        wait(dve, pT_mm, n - 1)
                    nc.vector.memset(waiter[:, 2 * (l % 2) + j:2 * (l % 2) + j + 1], 0.0)
                    for qt in range(2):
                        nc.vector.tensor_tensor_reduce(
                            out=s_sb[l % 2][:, j, qt, :], in0=psS[:, j, qt * 256:(qt + 1) * 256], in1=mask[:, qt, :],
                            scale=float(D) ** -0.5, scalar=-3e38, op0=ALU.add, op1=ALU.max,
                            accum_out=smax[:, l % 2, 2 * j + qt:2 * j + qt + 1]).then_inc(score_max, 1)
                wait(dve, score_max, 4 * n + 4)
                nc.vector.tensor_scalar(nmax[:, l % 2, :], smax[:, l % 2, :], -1.0, None,
                                        ALU.mult).then_inc(nmax_done, 1)

            def normalise_probs(n, l):
                wait(dve, exp_done, 4 * n + 4)
                nc.vector.reciprocal(rinv[:, l % 2, :], rsum[:, l % 2, :]).then_inc(rinv_done, 1)
                wait(dve, rinv_done, n + 1)
                for i in range(4):
                    p = s_sb[l % 2][:, i // 2, i % 2, :]
                    nc.vector.tensor_scalar(p, p, rinv[:, l % 2, i:i + 1], None, ALU.mult).then_inc(prob_done, 1)

            kv_low(1, k_hi[0][:], k_lo[0][:])
            for h in range(HPG):
                q_low(h + 1, 0, h)
                if h == 1:
                    kv_low(2, v_hi[0][:].rearrange("p t d -> p (t d)"), v_lo[0][:].rearrange("p t d -> p (t d)"))
            row_max(0, 0)
            normalise_probs(0, 0)
            dve.wait_ge(acc_zeroed, 1)

            def add_tile(m, lm):
                wait(dve, w_mm, m + 1)
                nc.vector.tensor_tensor(acc[:, lm, :], acc[:, lm, :], psW[:], ALU.add).then_inc(w_added, 1)

            def steps(g, first, last):
                for l in range(STEPS):
                    n = STEPS * g + l
                    par, s = l // 4, l % 4
                    if not (last and l == STEPS - 1):
                        row_max(n + 1, (l + 1) % STEPS)
                    if not (last and par == 1):
                        q_low(n + 5, 1 - par, s)
                        if s == 0:
                            kv_low(4 * g + 2 * par + 3, k_hi[1 - par][:], k_lo[1 - par][:])
                        if s == 1:
                            kv_low(4 * g + 2 * par + 4, v_hi[1 - par][:].rearrange("p t d -> p (t d)"),
                                   v_lo[1 - par][:].rearrange("p t d -> p (t d)"))
                    if not (last and l == STEPS - 1):
                        normalise_probs(n + 1, (l + 1) % STEPS)
                    wait(dve, pT_hi_done, n + 1)
                    nc.vector.tensor_tensor(pT_lo[:], psT[:].rearrange("p a b -> p (a b)")[:, 0:768], fp(pT_hi[:]),
                                            ALU.subtract).then_inc(pT_lo_done, 1)
                    if not (first and l < 2):
                        add_tile(n - 2, (l - 2) % STEPS)
                    wait(dve, o_hi_done, n + 1)
                    b_in, hp = s // 2, l % 2
                    nc.vector.tensor_tensor(o_lo[:, b_in, 2 * hp:2 * hp + 2, :],
                                            psO[:].rearrange("p (j q) -> p j q", j=2),
                                            fp(o_hi[:, b_in, 2 * hp:2 * hp + 2, :]), ALU.subtract).then_inc(o_lo_done, 1)

            groups(dve, steps)
            add_tile(NSTEP - 2, 6)
            add_tile(NSTEP - 1, 7)
            dve.wait_ge(w_added, NSTEP)

            dve.wait_ge(x1_landed, 16)
            for t in range(TILES):
                stats(acc[:, t, :], t, TILES + t + 1)
            add_eps(0, TILES, 2 * TILES, 3)
            invert(0, TILES, 3)
            for t in range(TILES):
                normalise(acc[:, t, :], acc[:, t, :], t).then_inc(norm_step, 1)
            for t in range(TILES):
                dve.wait_ge(norm_step, t + 1)
                nc.vector.tensor_tensor(x1[:, t, :], x1[:, t, :], acc[:, t, :], ALU.add).then_inc(norm_step, 1)
            for t in range(TILES):
                dve.wait_ge(norm_step, TILES + t + 1)
                stats(x1[:, t, :], t, 2 * TILES + t + 1)
            add_eps(0, TILES, 3 * TILES, 4)
            invert(0, TILES, 4)
            for t in range(TILES):
                wait(dve, turn_mm, TILES + t - 1)
                normalise(xn[:, t % 2, :], x1[:, t, :], t).then_inc(xn_done, 1)
                if t >= 1:
                    turned(t - 1, TILES + t)
            turned(TILES - 1, 2 * TILES)

            done = [0]

            def then(ins):
                done[0] += 1
                ins.then_inc(router_step, 1)
                dve.wait_ge(router_step, done[0])

            def spread(t):
                return t[:].rearrange("p (t a) -> p t a", a=1).to_broadcast([P, TILES, NE])

            dve.wait_ge(router_mm, 1)
            logits = psT[:, 0, 0:TILES * NE].rearrange("p (t e) -> p t e", t=TILES)
            then(nc.vector.tensor_reduce(top1[:], logits, AX_X, ALU.max))
            then(nc.vector.tensor_tensor(probs[:], logits, spread(top1), ALU.subtract))
            nc.vector.memset(comb[:, NE:NX, :], 1.0).then_inc(router_step, 1)
            done[0] += 1
            for e in range(NE):
                nc.vector.memset(rank[:, :, e:e + 1], float(NE - e)).then_inc(router_step, 1)
            done[0] += NE
            dve.wait_ge(router_exp, 1)
            then(nc.vector.tensor_reduce(tsum[:], probs[:], AX_X, ALU.add))
            then(nc.vector.reciprocal(tinv[:], tsum[:]))
            then(nc.vector.tensor_tensor(probs[:], probs[:], spread(tinv), ALU.mult))
            then(nc.vector.tensor_copy(left[:], probs[:]))
            for best, chosen in ((top1, first), (top2, second)):
                then(nc.vector.tensor_reduce(best[:], left[:], AX_X, ALU.max))
                then(nc.vector.tensor_tensor(chosen[:], left[:], spread(best), ALU.is_equal))
                then(nc.vector.tensor_tensor(chosen[:], chosen[:], rank[:], ALU.mult))
                then(nc.vector.tensor_reduce(low[:], chosen[:], AX_X, ALU.max))
                then(nc.vector.tensor_tensor(chosen[:], rank[:], spread(low), ALU.is_equal))
                then(nc.vector.scalar_tensor_tensor(out=left[:], in0=chosen[:], scalar=-2.0, in1=left[:],
                                                    op0=ALU.mult, op1=ALU.add))
            then(nc.vector.tensor_tensor(tsum[:], top1[:], top2[:], ALU.add))
            then(nc.vector.reciprocal(tinv[:], tsum[:]))
            then(nc.vector.tensor_tensor(first[:], first[:], second[:], ALU.add))
            then(nc.vector.tensor_tensor(first[:], first[:], probs[:], ALU.mult))
            then(nc.vector.tensor_tensor(comb[:, 0:NE, :].rearrange("p e t -> p t e"), first[:], spread(tinv), ALU.mult))
            dve.wait_ge(acc2_zeroed, 1)

            def hidden(w, th):
                wait(dve, silu_done, w + 1)
                wait(dve, u_mm, w + 1)
                nc.vector.tensor_tensor(hid[th][:], silu[th][:], bank_up[th], ALU.mult).then_inc(hid_done, 1)
                wait(dve, hid_hi_done, w + 1)
                nc.vector.tensor_tensor(hid_lo[th][:], hid[th][:], fp(hid_hi[th][:]),
                                        ALU.subtract).then_inc(hid_lo_done, 1)

            def add_down(w, th, j, first):
                for i in range(4):
                    t = 4 * th + i
                    wait(dve, d_mm, 4 * w + i + 1)
                    nc.vector.scalar_tensor_tensor(out=acc2[:, t, :], in0=bank_down[i], scalar=comb_e[:, j, t:t + 1],
                                                   in1=acc2[:, t, :], op0=ALU.mult, op1=ALU.add).then_inc(d_added, 1)

            def pair_units(i, first):
                for j in range(2):
                    for th in range(2):
                        w = 4 * i + 2 * j + th
                        hidden(w, th)
                        if not (first and j == 0 and th == 0):
                            pj, pth = (j, 0) if th == 1 else (1 - j, 1)
                            if pth == 0:
                                wait(dve, comb_e_done, 2 * i + j + 1)
                            add_down(w - 1, pth, pj, first)
                        if th == 0:
                            nc.vector.tensor_copy(comb_e[:, j, :].rearrange("p (a t) -> p a t", a=1),
                                                  comb[:, bass.ds(2 * i + j, 1), :]).then_inc(comb_e_done, 1)

            pair_units(0, True)
            with dve.Fori(1, NX // 2) as i:
                pair_units(i, False)
            add_down(UNITS - 1, 1, 1, False)
            dve.wait_ge(d_added, 4 * UNITS)

            for t in range(TILES):
                stats(acc2[:, t, :], t, 3 * TILES + t + 1)
            add_eps(0, TILES, 4 * TILES, 5)
            invert(0, TILES, 5)
            for t in range(TILES):
                normalise(acc2[:, t, :], acc2[:, t, :], t).then_inc(y_step, 1)
            for t in range(TILES):
                dve.wait_ge(y_step, t + 1)
                nc.vector.tensor_tensor(acc2[:, t, :], acc2[:, t, :], x1[:, t, :], ALU.add).then_inc(y_done, 1)

        @block.scalar
        def _(act):
            def copy(dst, src):
                return nc.scalar.activation(dst, src, ACT.Copy)

            def root(t0, t1, count):
                act.wait_ge(veps_done, count)
                nc.scalar.activation(std[:, t0:t1], veps[:, t0:t1], ACT.Sqrt).then_inc(std_done, 1)

            act.wait_ge(wl_landed, 16)
            for c in range(CH):
                copy(wl_hi[:, c, :], wl_raw[:, c, :]).then_inc(wl_hi_done, 1)
            root(0, 4, 1)

            def turned(t, count):
                act.wait_ge(turn_mm, count)
                copy(xT_hi[:, :, t * P:(t + 1) * P],
                     bank_turn[t % 2].rearrange("p (c q) -> p c q", c=CH)).then_inc(xT_hi_done, 1)

            root(4, 8, 2)
            for t in range(TILES):
                turned(t, t + 1)

            for j in range(8):
                act.wait_ge(lat_mm, j + 1)
                half, hp = j // 4, j % 4
                src = bank_lat[j % 3][0:64, :].rearrange("p (b t c r) -> p r c b t", b=2, t=32, c=4)
                for r in range(2):
                    dst = lat[64 * r:64 * r + 64, :, half * PAIR:(half + 1) * PAIR].rearrange(
                        "p c (b t) -> p c b t", b=2)[:, :, :, 2 * hp * 32:2 * hp * 32 + 32]
                    copy(dst, src[:, r]).then_inc(lat_even_done, 1)

            def kv_high(count, dst):
                wait(act, kv_mm, count)
                copy(dst, psKV[:]).then_inc(kv_hi_done, 1)

            def q_high(count, par, h):
                wait(act, q_mm, count)
                copy(q_hi[par][:, h, :], psQ[:]).then_inc(q_hi_done, 1)

            def exponentials(n, l):
                wait(act, nmax_done, n + 1)
                for i in range(4):
                    p = s_sb[l % 2][:, i // 2, i % 2, :]
                    nc.scalar.activation(p, p, ACT.Exp, bias=nmax[:, l % 2, i:i + 1],
                                         accum_out=rsum[:, l % 2, i:i + 1]).then_inc(exp_done, 1)

            kv_high(1, k_hi[0][:])
            for h in range(HPG):
                q_high(h + 1, 0, h)
                if h == 1:
                    kv_high(2, v_hi[0][:].rearrange("p t d -> p (t d)"))
            exponentials(0, 0)

            def steps(g, first, last):
                for l in range(STEPS):
                    n = STEPS * g + l
                    par, s = l // 4, l % 4
                    if not (last and l == STEPS - 1):
                        exponentials(n + 1, (l + 1) % STEPS)
                    if not (last and par == 1):
                        q_high(n + 5, 1 - par, s)
                        if s == 0:
                            kv_high(4 * g + 2 * par + 3, k_hi[1 - par][:])
                        if s == 1:
                            kv_high(4 * g + 2 * par + 4, v_hi[1 - par][:].rearrange("p t d -> p (t d)"))
                    wait(act, pT_mm, n + 1)
                    wait(act, o_mm, n)
                    copy(pT_hi[:], psT[:].rearrange("p a b -> p (a b)")[:, 0:768]).then_inc(pT_hi_done, 1)
                    wait(act, o_mm, n + 1)
                    b_in, hp = s // 2, l % 2
                    if not (first and l < 4):
                        wait(act, w_mm, n - 2 if hp == 0 else n - 3)
                    copy(o_hi[:, b_in, 2 * hp:2 * hp + 2, :],
                         psO[:].rearrange("p (j q) -> p j q", j=2)).then_inc(o_hi_done, 1)

            groups(act, steps)

            root(0, TILES, 3)
            root(0, TILES, 4)
            for t in range(TILES):
                turned(t, TILES + t + 1)
            act.wait_ge(router_step, 2)
            nc.scalar.activation(probs[:], probs[:], ACT.Exp).then_inc(router_exp, 1)

            def unit(w, th):
                wait(act, g_mm, w + 1)
                wait(act, hid_done, w - 1)
                nc.scalar.activation(silu[th][:], bank_gate[th], ACT.Silu).then_inc(silu_done, 1)
                wait(act, hid_done, w + 1)
                wait(act, d_mm, 4 * w - 4)
                copy(hid_hi[th][:], hid[th][:]).then_inc(hid_hi_done, 1)

            for w in range(4):
                unit(w, w % 2)
            with act.Fori(1, NX // 2) as i:
                for w in range(4):
                    unit(4 * i + w, w % 2)
            root(0, TILES, 5)


def kernel(L0_attn_hidden_states, L0_attn_Wq, L0_attn_Wk_down, L0_attn_Wv_down, L0_attn_Wk_up, L0_attn_Wv_up,
           L0_attn_Wo, L0_ffn_gate_w, L0_ffn_w_gate_up, L0_ffn_w_down, L0_ffn_shared_w_gate_up,
           L0_ffn_shared_w_down):
    import numpy as _np
    import concourse.bacc as _bacc
    from concourse import mybir as _mybir
    from concourse.bass_utils import run_bass_kernel_spmd as _run

    c = _np.ascontiguousarray
    heads = NG * HPG
    w_down_k = _np.asarray(L0_attn_Wk_down).reshape(NG, 32, HID)
    w_down_v = _np.asarray(L0_attn_Wv_down).reshape(NG, 32, HID)
    lat = _np.concatenate([w_down_k, w_down_v], axis=1).reshape(HID, CH, P)
    w_gu = _np.asarray(L0_ffn_w_gate_up).reshape(NE, 2, INTER, HID)
    s_gu = _np.asarray(L0_ffn_shared_w_gate_up).reshape(2, NX - NE, INTER, HID).transpose(1, 0, 2, 3)
    gu = _np.concatenate([w_gu, s_gu], axis=0).reshape(NX, 2 * INTER, CH, P)
    s_dn = _np.asarray(L0_ffn_shared_w_down).reshape(HID, NX - NE, INTER).transpose(1, 2, 0)
    up = _np.stack([_np.asarray(L0_attn_Wk_up), _np.asarray(L0_attn_Wv_up)]).reshape(2, NG, D, 2, P)
    arrays = {
        "x": c(_np.asarray(L0_attn_hidden_states).reshape(T, HID)),
        "w_lat": c(lat.transpose(2, 1, 0).reshape(P, CH * HID)),
        "w_q": c(_np.asarray(L0_attn_Wq).reshape(heads, D, CH, P).transpose(0, 3, 2, 1).reshape(heads, P, CH * D)),
        "w_o": c(_np.asarray(L0_attn_Wo).reshape(HID, heads, D).transpose(1, 2, 0)),
        "w_kv": c(up.transpose(1, 4, 0, 3, 2).reshape(NG, P, 4 * D)),
        "w_gate": c(_np.asarray(L0_ffn_gate_w).reshape(NE, CH, P).transpose(2, 1, 0).reshape(P, CH * NE)),
        "w_gu": c(gu.transpose(0, 3, 2, 1).reshape(NX, P, CH * 2 * INTER)),
        "w_dn": c(_np.concatenate([_np.asarray(L0_ffn_w_down).transpose(0, 2, 1), s_dn], axis=0)),
    }
    nc = _bacc.Bacc("TRN2", target_bir_lowering=False, num_devices=1)
    args = [nc.dram_tensor(n, a.shape, _mybir.dt.from_np(a.dtype), kind="ExternalInput").ap()
            for n, a in arrays.items()]
    args.append(nc.dram_tensor("out", (T, HID), _mybir.dt.float32, kind="ExternalOutput").ap())
    build_program(nc, *args)
    r = _run(nc, [arrays], core_ids=[0])
    return _np.asarray(r.results[0]["out"]).reshape(B, S, HID)
```

```python
from contextlib import ExitStack

import concourse.bass as bass
from concourse import mybir

ALU = mybir.AluOpType
ACT = mybir.ActivationFunctionType
AX_X = mybir.AxisListType.X
F32 = mybir.dt.float32
F32R = mybir.dt.float32r

P = 128
EPS = 1e-5
MASKED = -1e30

B, S, HID = 4, 256, 512
NG, HPG, D = 8, 4, 128
T = B * S
TILES = T // P
CH = HID // P
PAIR = 2 * S
STEPS = 8
NSTEP = NG * STEPS

NE, INTER, SHARED = 16, 128, 512
NX = NE + SHARED // INTER
HALF = 512
UNITS = 2 * NX


def build_program(nc, x, w_lat, w_q, w_o, w_kv, w_gate, w_gu, w_dn, out):
    x_tiles = x.rearrange("(t p) h -> p t h", p=P)
    out_tiles = out.rearrange("(t p) h -> p t h", p=P)

    top = ExitStack()
    with top:
        def sem(name):
            return top.enter_context(nc.semaphore(name))

        def allocate(stack):
            return lambda name, shape, dt=F32: stack.enter_context(nc.sbuf_tensor(name, shape, dt))

        psS = top.enter_context(nc.psum_tensor("psS", [P, 2, 512], F32))
        psT = top.enter_context(nc.psum_tensor("psT", [P, 2, 512], F32))
        psO = top.enter_context(nc.psum_tensor("psO", [P, 512], F32))
        psQ = top.enter_context(nc.psum_tensor("psQ", [P, 512], F32))
        psW = top.enter_context(nc.psum_tensor("psW", [P, 512], F32))
        psKV = top.enter_context(nc.psum_tensor("psKV", [P, 512], F32))
        bank_gate = [psS[:, 0, :], psS[:, 1, :]]
        bank_up = [psT[:, 0, :], psT[:, 1, :]]
        bank_down = [psO[:], psQ[:], psW[:], psKV[:]]
        bank_turn = [psS[:, t % 2, :] for t in range(TILES)]
        bank_turn += [psS[:, t % 2, :] if t < 4 else (psS if t % 2 == 0 else psT)[:, 1, :] for t in range(TILES)]
        bank_lat = [psT[:, 0, :], psT[:, 1, :], psO[:]]

        sb = allocate(top)
        ident = sb("ident", [P, P])
        mask = sb("mask", [P, 2, 256])
        zero = sb("zero", [P, 1])
        waiter = sb("waiter", [P, 4])
        xT_hi = sb("xT_hi", [P, CH, T], F32R)
        xT_lo = sb("xT_lo", [P, CH, T], F32R)
        acc = sb("acc", [P, TILES, HID])
        bn = sb("bn", [P, TILES, 6])
        mean_var = sb("mean_var", [P, TILES, 2])
        veps = sb("veps", [P, TILES])
        neg_half = sb("neg_half", [P, 2])
        neg_mean = sb("neg_mean", [P, TILES])
        rstd = sb("rstd", [P, TILES])
        shift = sb("shift", [P, TILES])
        smax = sb("smax", [P, 2, 4])
        nmax = sb("nmax", [P, 2, 4])
        rsum = sb("rsum", [P, 2, 4])
        rinv = sb("rinv", [P, 2, 4])

        attn = ExitStack()
        early = ExitStack()
        sa = allocate(early)
        x_in = sa("x_in", [P, TILES, HID])
        wl_raw = sa("wl_raw", [P, CH, HID])
        wl_hi = sa("wl_hi", [P, CH, HID], F32R)
        wl_lo = sa("wl_lo", [P, CH, HID], F32R)
        early.close()
        sa = allocate(attn)
        o_hi = sa("o_hi", [P, 2, HPG, S], F32R)
        o_lo = sa("o_lo", [P, 2, HPG, S], F32R)
        pT_hi = sa("pT_hi", [P, 768], F32R)
        pT_lo = sa("pT_lo", [P, 768], F32R)

        def pair_of(name, shape, dt=F32R):
            return sa(f"{name}_hi", shape, dt), sa(f"{name}_lo", shape, dt)

        s_sb1 = sa("s_sb1", [P, 2, 2, 256])
        k1, v1, q1 = pair_of("k1", [P, PAIR]), pair_of("v1", [P, 4, D]), pair_of("q1", [P, HPG, PAIR])
        s_sb0 = sa("s_sb0", [P, 2, 2, 256])
        k0, v0, q0 = pair_of("k0", [P, PAIR]), pair_of("v0", [P, 4, D]), pair_of("q0", [P, HPG, PAIR])
        s_sb = [s_sb0, s_sb1]
        (k_hi, k_lo), (v_hi, v_lo), (q_hi, q_lo) = zip(k0, k1), zip(v0, v1), zip(q0, q1)
        lat = sa("lat", [P, 4, T])
        raw = sa("raw", [P, 4, 512])
        wkv = sa("wkv", [P, 2, 2, D])
        wq_hi = sa("wq_hi", [P, HPG, CH, D], F32R)
        wq_lo = sa("wq_lo", [P, HPG, CH, D], F32R)
        wo_hi = sa("wo_hi", [P, 2, HPG, HID], F32R)
        wo_lo = sa("wo_lo", [P, 2, HPG, HID], F32R)
        attn.close()

        ffn = ExitStack()
        sf = allocate(ffn)
        acc2 = sf("acc2", [P, TILES, HID])
        silu = [sf(f"silu{i}", [P, HALF]) for i in range(2)]
        hid = [sf(f"hid{i}", [P, HALF]) for i in range(2)]
        hid_hi = [sf(f"hid_hi{i}", [P, HALF], F32R) for i in range(2)]
        hid_lo = [sf(f"hid_lo{i}", [P, HALF], F32R) for i in range(2)]
        comb = sf("comb", [P, NX, TILES])
        comb_e = sf("comb_e", [P, 2, TILES])
        sf("fill_a", [P, 2 * 256 - NX * TILES - 2 * TILES])
        gu_hi, gu_lo, dn_hi, dn_lo, gu_raw, dn_raw = {}, {}, {}, {}, {}, {}

        def cut_weights(j):
            gu_hi[j] = sf(f"gu_hi{j}", [P, CH, 256], F32R)
            gu_lo[j] = sf(f"gu_lo{j}", [P, CH, 256], F32R)
            dn_hi[j] = sf(f"dn_hi{j}", [P, HID], F32R)
            dn_lo[j] = sf(f"dn_lo{j}", [P, HID], F32R)

        cut_weights(1)
        sf("fill_b", [P, 8 * 256])
        cut_weights(0)
        for j in range(2):
            gu_raw[j] = sf(f"gu_raw{j}", [P, CH, 256])
            dn_raw[j] = sf(f"dn_raw{j}", [P, HID])
        w_g = sf("w_g", [P, CH, NE])
        probs = sf("probs", [P, TILES, NE])
        left = sf("left", [P, TILES, NE])
        first = sf("first", [P, TILES, NE])
        second = sf("second", [P, TILES, NE])
        rank = sf("rank", [P, TILES, NE])
        top1 = sf("top1", [P, TILES])
        top2 = sf("top2", [P, TILES])
        low = sf("low", [P, TILES])
        tsum = sf("tsum", [P, TILES])
        tinv = sf("tinv", [P, TILES])
        sf("fill_c", [P, 16 * 256 - CH * NE - 5 * TILES * NE - 5 * TILES])
        xn = sf("xn", [P, 4, HID])
        sf("fill_d", [P, 2 * 256])
        x1 = sf("x1", [P, TILES, HID])
        ffn.close()

        x_in_landed = [sem(f"x_in_landed{i}") for i in range(4)]
        wl_landed = sem("wl_landed")
        raw_landed = [sem(f"raw_landed{i}") for i in range(4)]
        wkv_landed = sem("wkv_landed")
        x1_landed = sem("x1_landed")
        gate_landed = sem("gate_landed")
        gu_landed = [sem(f"gu_landed{i}") for i in range(2)]
        dn_landed = [sem(f"dn_landed{i}") for i in range(2)]
        out_stored = sem("out_stored")
        const_step = sem("const_step")
        consts_ready = sem("consts_ready")
        acc_zeroed = sem("acc_zeroed")
        bn_done = sem("bn_done")
        aggr_done = sem("aggr_done")
        veps_done = sem("veps_done")
        rstd_done = sem("rstd_done")
        shift_done = sem("shift_done")
        normed = sem("normed")
        x1_added = sem("x1_added")
        turn_mm = sem("turn_mm")
        xT_hi_done = sem("xT_hi_done")
        xT_lo_done = sem("xT_lo_done")
        wl_hi_done = sem("wl_hi_done")
        wl_lo_done = sem("wl_lo_done")
        lat_mm = sem("lat_mm")
        lat_even_done = sem("lat_even_done")
        lat_odd_done = sem("lat_odd_done")
        wq_hi_done = sem("wq_hi_done")
        wq_cut = sem("wq_cut")
        wo_hi_done = sem("wo_hi_done")
        wo_cut = sem("wo_cut")
        score_mm = sem("score_mm")
        score_max = sem("score_max")
        nmax_done = sem("nmax_done")
        exp_done = sem("exp_done")
        rinv_done = sem("rinv_done")
        prob_done = sem("prob_done")
        pT_mm = sem("pT_mm")
        pT_hi_done = sem("pT_hi_done")
        pT_lo_done = sem("pT_lo_done")
        o_mm = sem("o_mm")
        o_hi_done = sem("o_hi_done")
        o_lo_done = sem("o_lo_done")
        q_mm = sem("q_mm")
        q_hi_done = sem("q_hi_done")
        q_lo_done = sem("q_lo_done")
        kv_mm = sem("kv_mm")
        kv_hi_done = sem("kv_hi_done")
        kv_lo_done = sem("kv_lo_done")
        w_mm = sem("w_mm")
        w_added = sem("w_added")
        router_mm = sem("router_mm")
        router_exp = sem("router_exp")
        router_step = sem("router_step")
        gu_hi_done = sem("gu_hi_done")
        gu_cut = sem("gu_cut")
        dn_hi_done = sem("dn_hi_done")
        dn_cut = sem("dn_cut")
        g_mm = sem("g_mm")
        u_mm = sem("u_mm")
        silu_done = sem("silu_done")
        hid_done = sem("hid_done")
        hid_hi_done = sem("hid_hi_done")
        hid_lo_done = sem("hid_lo_done")
        d_mm = sem("d_mm")
        d_added = sem("d_added")
        comb_e_done = sem("comb_e_done")
        y_added_dve = sem("y_added_dve")
        y_added_pool = sem("y_added_pool")

        def fp(t):
            return t.bitcast(F32)

        def wait(eng, s, value):
            if not (isinstance(value, int) and value <= 0):
                eng.wait_ge(s, value)

        order = [("x", p) for p in range(4)]
        order += [("a", 0), ("a", 1), ("b", 0), ("a", 2), ("b", 1), ("a", 3), ("b", 2), ("b", 3)]
        order += [("y", p) for p in range(4)]
        nth = {what: i for i, what in enumerate(order)}
        norm_order = [("x", p) for p in range(4)]
        norm_order += [("a", 0), ("a", 1), ("b", 0), ("a", 2), ("b", 1), ("a", 3), ("b", 2), ("b", 3)]
        norm_order += [("y", p) for p in range(4)]
        norm_nth = {what: i for i, what in enumerate(norm_order)}

        def groups(eng, body):
            body(0, True, False)
            with eng.Fori(1, NG - 1) as g:
                body(g, False, False)
            body(NG - 1, False, True)


        block = top.enter_context(nc.Block())

        @block.sync
        def _(sp):
            for i in range(4):
                sp.dma_start(x_in[:, 2 * i:2 * i + 2, :], x_tiles[:, 2 * i:2 * i + 2, :]).then_inc(x_in_landed[i], 16)
                if i == 0:
                    sp.dma_start(wl_raw[:], w_lat.rearrange("p (c n) -> p c n", c=CH)).then_inc(wl_landed, 16)

            def pieces(g, first, last):
                if first:
                    sp.dma_start(wkv[:], w_kv[0].rearrange("p (a c d) -> p a c d", a=2, c=2)).then_inc(wkv_landed, 16)
                kinds = ((w_q, wq_cut), (w_o, wo_cut))
                turns = [(h, kind) for h in range(HPG) for kind in range(2)]
                for h, kind in sorted(turns, key=lambda turn: turn[1]) if first else turns:
                    weights, cut = kinds[kind]
                    slot = 2 * (h % 2) + kind
                    if not (first and h < 2):
                        wait(sp, cut, 4 * g + h - 1)
                    sp.dma_start(raw[:, slot, :], weights[HPG * g + h]).then_inc(raw_landed[slot], 16)
                if not first:
                    wait(sp, kv_mm, 4 * g)
                    sp.dma_start(wkv[:], w_kv[g].rearrange("p (a c d) -> p a c d", a=2, c=2)).then_inc(wkv_landed, 16)

            groups(sp, pieces)

            sp.wait_ge(q_mm, NSTEP)
            sp.dma_start(x1[:], x_tiles).then_inc(x1_landed, 16)
            sp.wait_ge(kv_mm, 4 * NG)
            sp.dma_start(w_g[:], w_gate.rearrange("p (c e) -> p c e", c=CH)).then_inc(gate_landed, 16)
            sp.wait_ge(o_mm, NSTEP - 4)

            def expert(e, j, first):
                if not first:
                    wait(sp, gu_cut, e - 1)
                sp.dma_start(gu_raw[j][:], w_gu[e].rearrange("p (c n) -> p c n", c=CH)).then_inc(gu_landed[j], 16)
                if not first:
                    wait(sp, dn_cut, e - 1)
                sp.dma_start(dn_raw[j][:], w_dn[e]).then_inc(dn_landed[j], 16)

            expert(0, 0, True)
            expert(1, 1, True)
            with sp.Fori(1, NX // 2) as pair:
                expert(2 * pair, 0, False)
                expert(2 * pair + 1, 1, False)

            for t in range(TILES):
                if t < 4:
                    sp.wait_ge(y_added_pool, t + 1)
                else:
                    sp.wait_ge(y_added_dve, t - 3)
                sp.dma_start(out_tiles[:, t, :], acc2[:, t, :]).then_inc(out_stored, 16)
            sp.wait_ge(out_stored, 16 * TILES)

        @block.gpsimd
        def _(pool):
            nc.gpsimd.memset(ident[:], 0.0).then_inc(const_step, 1)
            nc.gpsimd.memset(neg_half[:], -0.5).then_inc(const_step, 1)
            nc.gpsimd.memset(zero[:], 0.0).then_inc(const_step, 1)
            pool.wait_ge(const_step, 3)
            nc.gpsimd.affine_select(out=ident[:], in_=ident[:], compare_op=ALU.not_equal, fill=1.0, base=0,
                                    pattern=[[-1, P]], channel_multiplier=1).then_inc(consts_ready, 1)

            def scale_and_shift(what):
                i, t = nth[what], 2 * what[1]
                pool.wait_ge(aggr_done, 2 * i + 2)
                nc.gpsimd.tensor_scalar(veps[:, t:t + 2], mean_var[:, t:t + 2, 1], EPS, None,
                                        ALU.add).then_inc(veps_done, 1)
                nc.gpsimd.tensor_scalar(neg_mean[:, t:t + 2], mean_var[:, t:t + 2, 0], -1.0, None,
                                        ALU.mult).then_inc(veps_done, 1)
                pool.wait_ge(veps_done, 2 * i + 2)
                nc.gpsimd.tensor_tensor(rstd[:, t:t + 2], veps[:, t:t + 2], neg_half[:], ALU.pow).then_inc(rstd_done, 1)
                pool.wait_ge(rstd_done, i + 1)
                nc.gpsimd.tensor_tensor(shift[:, t:t + 2], neg_mean[:, t:t + 2], rstd[:, t:t + 2],
                                        ALU.mult).then_inc(shift_done, 1)

            def latent_low(c):
                pool.wait_ge(wl_hi_done, c + 1)
                nc.gpsimd.tensor_tensor(wl_lo[:, c, :], wl_raw[:, c, :], fp(wl_hi[:, c, :]),
                                        ALU.subtract).then_inc(wl_lo_done, 1)

            scale_and_shift(("x", 0))
            latent_low(0)
            scale_and_shift(("x", 1))
            for c in range(1, CH):
                latent_low(c)
            scale_and_shift(("x", 2))
            scale_and_shift(("x", 3))

            def round_to(dst, src):
                z = zero[:]
                for n in src.shape[2:]:
                    z = z.rearrange("p (a b) -> p a b", b=1) if len(z.shape) < len(src.shape) else z
                return nc.gpsimd.tensor_tensor(dst, src, z.to_broadcast(list(src.shape)), ALU.add)

            def cut_queries(g, h, first):
                if not first:
                    wait(pool, q_mm, 8 * g + h - 3)
                wait(pool, raw_landed[2 * (h % 2)], 32 * g + 16 * (h // 2) + 16)
                src = raw[:, 2 * (h % 2), :].rearrange("p (c d) -> p c d", c=CH)
                round_to(wq_hi[:, h], src).then_inc(wq_hi_done, 1)
                wait(pool, wq_hi_done, 4 * g + h + 1)
                nc.gpsimd.tensor_tensor(wq_lo[:, h], src, fp(wq_hi[:, h]), ALU.subtract).then_inc(wq_cut, 1)

            def cut_outputs(g, h, first):
                if first:
                    pool.wait_ge(lat_mm, 8)
                elif h == 0:
                    wait(pool, w_mm, 8 * g - 8)
                wait(pool, raw_landed[2 * (h % 2) + 1], 32 * g + 16 * (h // 2) + 16)
                src = raw[:, 2 * (h % 2) + 1, :]
                slot = g % 2
                round_to(wo_hi[:, slot, h], src).then_inc(wo_hi_done, 1)
                wait(pool, wo_hi_done, 4 * g + h + 1)
                nc.gpsimd.tensor_tensor(wo_lo[:, slot, h], src, fp(wo_hi[:, slot, h]),
                                        ALU.subtract).then_inc(wo_cut, 1)

            def cut(g, first, last):
                if not first:
                    for h in range(HPG):
                        cut_queries(g, h, False)
                        cut_outputs(g, h, False)
                    return
                cut_queries(0, 0, True)
                nc.gpsimd.memset(mask[:], 0.0).then_inc(const_step, 1)
                pool.wait_ge(const_step, 4)
                for t in range(2):
                    nc.gpsimd.affine_select(out=mask[:, t, :], in_=mask[:, t, :], compare_op=ALU.is_ge, fill=MASKED,
                                            base=P * t, pattern=[[-1, 256]],
                                            channel_multiplier=1).then_inc(consts_ready, 1)
                for h in range(1, HPG):
                    cut_queries(0, h, True)
                nc.gpsimd.memset(acc[:], 0.0).then_inc(acc_zeroed, 1)
                for h in range(HPG):
                    cut_outputs(0, h, True)

            groups(pool, cut)
            nc_mid = [what for what in order if what[0] in "ab"]
            for what in nc_mid[:3]:
                scale_and_shift(what)

            pool.wait_ge(o_mm, NSTEP - 4)

            def expert(i, j, first):
                e = 2 * i + j
                wait(pool, gu_landed[j], 16 * i + 16)
                if not first:
                    wait(pool, u_mm, 2 * e - 2)
                round_to(gu_hi[j][:], gu_raw[j][:]).then_inc(gu_hi_done, 1)
                wait(pool, gu_hi_done, e + 1)
                nc.gpsimd.tensor_tensor(gu_lo[j][:], gu_raw[j][:], fp(gu_hi[j][:]), ALU.subtract).then_inc(gu_cut, 1)
                wait(pool, dn_landed[j], 16 * i + 16)
                if not first:
                    wait(pool, d_mm, 8 * e - 8)
                round_to(dn_hi[j][:], dn_raw[j][:]).then_inc(dn_hi_done, 1)
                wait(pool, dn_hi_done, e + 1)
                nc.gpsimd.tensor_tensor(dn_lo[j][:], dn_raw[j][:], fp(dn_hi[j][:]), ALU.subtract).then_inc(dn_cut, 1)

            expert(0, 0, True)
            for what in nc_mid[3:]:
                scale_and_shift(what)
            pool.wait_ge(score_mm, 2 * NSTEP)
            expert(0, 1, True)
            with pool.Fori(1, NX // 2) as pair:
                expert(pair, 0, False)
                expert(pair, 1, False)

            for p in range(4):
                scale_and_shift(("y", p))
            for t in range(4):
                pool.wait_ge(normed, 2 * norm_nth["y", 0] + t + 1)
                nc.gpsimd.tensor_tensor(acc2[:, t, :], acc2[:, t, :], x1[:, t, :], ALU.add).then_inc(y_added_pool, 1)

        @block.tensor
        def _(pe):
            def three(dst, hi_l, lo_l, hi_r, lo_r, start, stop):
                nc.tensor.matmul(dst, hi_l, hi_r, start=start, stop=False)
                nc.tensor.matmul(dst, hi_l, lo_r, start=False, stop=False)
                return nc.tensor.matmul(dst, lo_l, hi_r, start=False, stop=stop)

            def turn(i, src):
                for c in range(CH):
                    mm = nc.tensor.transpose(bank_turn[i][:, c * P:(c + 1) * P], src[:, c * P:(c + 1) * P], ident[:])
                mm.then_inc(turn_mm, 1)

            pe.wait_ge(consts_ready, 1)
            for t in range(4):
                pe.wait_ge(normed, t + 1)
                wait(pe, xT_lo_done, t - 1)
                turn(t, x_in[:, t, :])

            def latents(j):
                half, hp = j // 4, j % 4
                pe.wait_ge(xT_lo_done, 4 * half + 4)
                wait(pe, lat_even_done, 2 * (j - 2))
                wait(pe, lat_odd_done, 2 * (j - 2))
                rows = slice(hp * P, (hp + 1) * P)
                cols = slice(half * PAIR, (half + 1) * PAIR)
                for c in range(CH):
                    if j == 0:
                        pe.wait_ge(wl_lo_done, c + 1)
                    mm = three(bank_lat[j % 3], wl_hi[:, c, rows], wl_lo[:, c, rows],
                               xT_hi[:, c, cols], xT_lo[:, c, cols], c == 0, c == CH - 1)
                mm.then_inc(lat_mm, 1)

            for j in range(4):
                latents(j)
                t = 4 + j
                pe.wait_ge(normed, t + 1)
                wait(pe, xT_lo_done, t - 1)
                turn(t, x_in[:, t, :])

            def keys(u, par):
                for c in range(2):
                    mm = nc.tensor.matmul(psKV[:], wkv[:, 0, c, :], lat[:, c, par * PAIR:(par + 1) * PAIR],
                                          start=c == 0, stop=c == 1)
                mm.then_inc(kv_mm, 1)

            def values(u, par):
                for t in range(4):
                    for c in range(2):
                        mm = nc.tensor.matmul(psKV[:, t * D:(t + 1) * D],
                                              lat[:, 2 + c, par * PAIR + t * P:par * PAIR + (t + 1) * P],
                                              wkv[:, 1, c, :], start=c == 0, stop=c == 1)
                mm.then_inc(kv_mm, 1)

            def queries(h, par):
                for c in range(CH):
                    mm = three(psQ[:], wq_hi[:, h, c, :], wq_lo[:, h, c, :],
                               xT_hi[:, c, par * PAIR:(par + 1) * PAIR], xT_lo[:, c, par * PAIR:(par + 1) * PAIR],
                               c == 0, c == CH - 1)
                mm.then_inc(q_mm, 1)

            def scores(n, l):
                par, b_in, hp = l // 4, l % 4 // 2, l % 2
                u_done = 4 * (n // 4) if isinstance(n, int) else n - l % 4
                wait(pe, kv_lo_done, 2 * (n // 4) + 1 if isinstance(n, int) else (n - l % 4) // 2 + 1)
                wait(pe, q_lo_done, u_done + 2 * hp + 2)
                for j in range(2):
                    h = 2 * hp + j
                    wait(pe, score_max, 4 * n - 2 + 2 * j)
                    for qt in range(2):
                        at = slice(b_in * S + qt * P, b_in * S + (qt + 1) * P)
                        ks = slice(b_in * S, (b_in + 1) * S)
                        mm = three(psS[:, j, qt * 256:(qt + 1) * 256], q_hi[par][:, h, at], q_lo[par][:, h, at],
                                   k_hi[par][:, ks], k_lo[par][:, ks], True, True)
                    mm.then_inc(score_mm, 1)

            def turn_probs(n, l):
                wait(pe, prob_done, 4 * n + 4)
                wait(pe, pT_lo_done, n)
                p_sb = s_sb[l % 2]
                for j in range(2):
                    for qt in range(2):
                        nc.tensor.transpose(psT[:, 0, j * 256 + qt * P:j * 256 + (qt + 1) * P],
                                            p_sb[:, j, qt, 0:P], ident[:])
                    mm = nc.tensor.transpose(psT[:, 1, j * P:(j + 1) * P], p_sb[:, j, 1, P:2 * P], ident[:])
                mm.then_inc(pT_mm, 1)

            def attend(n, l):
                par, b_in = l // 4, l % 4 // 2
                wait(pe, pT_lo_done, n + 1)
                if l % 4 == 0:
                    wait(pe, kv_lo_done, n // 2 + 2 if isinstance(n, int) else n // 2 + 2)
                wait(pe, o_lo_done, n)
                v0, v1 = 2 * b_in, 2 * b_in + 1
                three(psO[:], v_hi[par][:, v0, :], v_lo[par][:, v0, :], pT_hi[:, 0:512], pT_lo[:, 0:512], True, False)
                late = psO[:].rearrange("p (j q) -> p j q", j=2)[:, :, P:2 * P]
                mm = three(late, v_hi[par][:, v1, :], v_lo[par][:, v1, :],
                           pT_hi[:, 512:768].rearrange("p (j q) -> p j q", j=2),
                           pT_lo[:, 512:768].rearrange("p (j q) -> p j q", j=2), False, True)
                mm.then_inc(o_mm, 1)

            def project(m, lm, slot):
                b_in, tt = lm % 4 // 2, lm % 2
                wait(pe, o_lo_done, m - tt + 2)
                wait(pe, w_added, m)
                for h in range(HPG):
                    at = slice(tt * P, (tt + 1) * P)
                    mm = three(psW[:], o_hi[:, b_in, h, at], o_lo[:, b_in, h, at],
                               wo_hi[:, slot, h, :], wo_lo[:, slot, h, :], h == 0, h == HPG - 1)
                mm.then_inc(w_mm, 1)

            pe.wait_ge(wkv_landed, 16)
            pe.wait_ge(lat_even_done, 8)
            pe.wait_ge(lat_odd_done, 8)
            keys(0, 0)
            for h in range(HPG):
                pe.wait_ge(wq_cut, h + 1)
                wait(pe, q_lo_done, h)
                queries(h, 0)
                if h == 0:
                    pe.wait_ge(kv_lo_done, 1)
                    values(0, 0)
                if h == 1:
                    scores(0, 0)
                if h > 1:
                    latents(2 + h)
            latents(6)
            latents(7)
            pe.wait_ge(lat_even_done, 16)
            pe.wait_ge(lat_odd_done, 16)

            def steps(g, first, last):
                for l in range(STEPS):
                    n = STEPS * g + l
                    par, s = l // 4, l % 4
                    if not (last and l == STEPS - 1):
                        scores(n + 1, (l + 1) % STEPS)
                    turn_probs(n, l)
                    if not (last and par == 1):
                        wait(pe, wq_cut, 4 * g + s + 1 + 4 * par)
                        wait(pe, q_lo_done, n + 4)
                        queries(s, 1 - par)
                        if s < 2:
                            if s == 0 and par == 1:
                                wait(pe, wkv_landed, 16 * g + 32)
                            wait(pe, kv_lo_done, (4 * g + 2 * par + 2) + s)
                            (keys if s == 0 else values)(None, 1 - par)
                    if not (first and l < 2):
                        lm = (l - 2) % STEPS
                        if l == 2:
                            wait(pe, wo_cut, 4 * g + 4)
                        project(n - 2, lm, (g if l >= 2 else g + 1) % 2)
                    attend(n, l)

            groups(pe, steps)
            project(NSTEP - 2, 6, (NG - 1) % 2)
            project(NSTEP - 1, 7, (NG - 1) % 2)

            def logits(t):
                pe.wait_ge(xT_lo_done, TILES + t + 1)
                for c in range(CH):
                    for part, x_part in enumerate((xT_hi, xT_lo)):
                        mm = nc.tensor.matmul(psKV[:, t * NE:(t + 1) * NE], fp(x_part[:, c, t * P:(t + 1) * P]),
                                              w_g[:, c, :], start=c == 0 and part == 0, stop=c == CH - 1 and part == 1)
                return mm

            def gate_up(w, e, th, j, first):
                if th == 0:
                    wait(pe, gu_cut, e + 1)
                if not first:
                    wait(pe, silu_done, w - 1)
                cols = slice(th * HALF, (th + 1) * HALF)
                for c in range(CH):
                    mm = three(bank_gate[th], gu_hi[j][:, c, 0:P], gu_lo[j][:, c, 0:P],
                               xT_hi[:, c, cols], xT_lo[:, c, cols], c == 0, c == CH - 1)
                mm.then_inc(g_mm, 1)
                if not first:
                    wait(pe, hid_done, w - 1)
                for c in range(CH):
                    mm = three(bank_up[th], gu_hi[j][:, c, P:2 * P], gu_lo[j][:, c, P:2 * P],
                               xT_hi[:, c, cols], xT_lo[:, c, cols], c == 0, c == CH - 1)
                mm.then_inc(u_mm, 1)

            def down(w, e, th, j, first):
                wait(pe, hid_lo_done, w + 1)
                if th == 0:
                    wait(pe, dn_cut, e + 1)
                for i in range(4):
                    if not first:
                        wait(pe, d_added, 4 * w + i - 3)
                    elif w == 0 and i == 3:
                        pe.wait_ge(router_step, 2)
                    at = slice(i * P, (i + 1) * P)
                    three(bank_down[i], hid_hi[th][:, at], hid_lo[th][:, at], dn_hi[j][:], dn_lo[j][:],
                          True, True).then_inc(d_mm, 1)

            for t in range(4):
                pe.wait_ge(normed, 2 * norm_nth["b", t // 2] + t % 2 + 1)
                wait(pe, score_max, 4 * NSTEP)
                wait(pe, xT_lo_done, TILES + t - 1)
                turn(TILES + t, xn[:, t % 4, :])
            pe.wait_ge(xT_lo_done, TILES + 4)
            pe.wait_ge(pT_lo_done, NSTEP)
            gate_up(0, 0, 0, 0, True)
            pe.wait_ge(gate_landed, 16)
            for t in range(4):
                logits(t)
            for t in range(4, TILES):
                pe.wait_ge(normed, 2 * norm_nth["b", t // 2] + t % 2 + 1)
                if t >= 6:
                    pe.wait_ge(xT_lo_done, TILES + t - 1)
                turn(TILES + t, xn[:, t % 4, :])
                if t % 2:
                    for tt in (t - 1, t):
                        mm = logits(tt)
            mm.then_inc(router_mm, 1)

            def pair_units(i, first):
                for j in range(2):
                    for th in range(2):
                        w = 4 * i + 2 * j + th
                        if not (first and w == 0):
                            gate_up(w, 2 * i + j, th, j, first and j == 0)
                        if not (first and j == 0 and th == 0):
                            pj, pth = (j, 0) if th == 1 else (1 - j, 1)
                            down(w - 1, 2 * i + j - (1 - th), pth, pj, first and j == 0)

            pair_units(0, True)
            with pe.Fori(1, NX // 2) as i:
                pair_units(i, False)
            down(UNITS - 1, NX - 1, 1, 1, False)

        @block.vector
        def _(dve):
            def stats(what, src):
                i, t = nth[what], 2 * what[1]
                for k in range(2):
                    nc.vector.bn_stats(bn[:, t + k, :], src[:, t + k, :]).then_inc(bn_done, 1)
                for k in range(2):
                    dve.wait_ge(bn_done, 2 * i + k + 1)
                    nc.vector.bn_aggr(mean_var[:, t + k, :], bn[:, t + k, :]).then_inc(aggr_done, 1)

            def turned(i):
                t = i % TILES
                dve.wait_ge(xT_hi_done, i + 1)
                nc.vector.tensor_tensor(xT_lo[:, :, t * P:(t + 1) * P],
                                        bank_turn[i].rearrange("p (c q) -> p c q", c=CH),
                                        fp(xT_hi[:, :, t * P:(t + 1) * P]), ALU.subtract).then_inc(xT_lo_done, 1)

            for p in range(4):
                dve.wait_ge(x_in_landed[p], 16)
                stats(("x", p), x_in)
            for t in range(4):
                turned(t)

            def latents(j, e, copy):
                half, hp = j // 4, j % 4
                src = bank_lat[j % 3][64 * e:64 * e + 64, :].rearrange("p (b t c r) -> p r c b t", b=2, t=32, c=4)
                for r in range(2):
                    dst = lat[64 * r:64 * r + 64, :, half * PAIR:(half + 1) * PAIR].rearrange(
                        "p c (b t) -> p c b t", b=2)[:, :, :, (2 * hp + e) * 32:(2 * hp + e) * 32 + 32]
                    copy(dst, src[:, r])

            def odd_latents(j):
                dve.wait_ge(lat_mm, j + 1)
                latents(j, 1, lambda d, s: nc.vector.tensor_copy(d, s).then_inc(lat_odd_done, 1))

            for j in range(4):
                odd_latents(j)
                turned(4 + j)

            def kv_low(count, dst_hi, dst_lo):
                wait(dve, kv_hi_done, count)
                nc.vector.tensor_tensor(dst_lo, psKV[:], fp(dst_hi), ALU.subtract).then_inc(kv_lo_done, 1)

            def q_low(count, par, h):
                wait(dve, q_hi_done, count)
                nc.vector.tensor_tensor(q_lo[par][:, h, :], psQ[:], fp(q_hi[par][:, h, :]),
                                        ALU.subtract).then_inc(q_lo_done, 1)

            def row_max(n, l):
                for j in range(2):
                    wait(dve, score_mm, 2 * n + j + 1)
                    if j == 0:
                        wait(dve, pT_mm, n - 1)
                    nc.vector.memset(waiter[:, 2 * (l % 2) + j:2 * (l % 2) + j + 1], 0.0)
                    for qt in range(2):
                        nc.vector.tensor_tensor_reduce(
                            out=s_sb[l % 2][:, j, qt, :], in0=psS[:, j, qt * 256:(qt + 1) * 256], in1=mask[:, qt, :],
                            scale=float(D) ** -0.5, scalar=-3e38, op0=ALU.add, op1=ALU.max,
                            accum_out=smax[:, l % 2, 2 * j + qt:2 * j + qt + 1]).then_inc(score_max, 1)
                wait(dve, score_max, 4 * n + 4)
                nc.vector.tensor_scalar(nmax[:, l % 2, :], smax[:, l % 2, :], -1.0, None,
                                        ALU.mult).then_inc(nmax_done, 1)

            def normalise_probs(n, l):
                wait(dve, exp_done, 4 * n + 4)
                nc.vector.reciprocal(rinv[:, l % 2, :], rsum[:, l % 2, :]).then_inc(rinv_done, 1)
                wait(dve, rinv_done, n + 1)
                for i in range(4):
                    p = s_sb[l % 2][:, i // 2, i % 2, :]
                    nc.vector.tensor_scalar(p, p, rinv[:, l % 2, i:i + 1], None, ALU.mult).then_inc(prob_done, 1)

            kv_low(1, k_hi[0][:], k_lo[0][:])
            for h in range(HPG):
                q_low(h + 1, 0, h)
                if h == 0:
                    kv_low(2, v_hi[0][:].rearrange("p t d -> p (t d)"), v_lo[0][:].rearrange("p t d -> p (t d)"))
                if h == 1:
                    row_max(0, 0)
                if h > 1:
                    odd_latents(2 + h)
            normalise_probs(0, 0)
            odd_latents(6)
            odd_latents(7)
            dve.wait_ge(acc_zeroed, 1)

            def attn_stats(p):
                dve.wait_ge(w_added, NSTEP - 8 + 2 * p + 2)
                stats(("a", p), acc)

            def residual(p):
                dve.wait_ge(x1_landed, 16)
                for k in range(2):
                    t = 2 * p + k
                    dve.wait_ge(normed, 2 * norm_nth["a", p] + k + 1)
                    nc.vector.tensor_tensor(x1[:, t, :], x1[:, t, :], acc[:, t, :], ALU.add).then_inc(x1_added, 1)
                dve.wait_ge(x1_added, 2 * p + 2)
                stats(("b", p), x1)

            def add_tile(m, lm):
                wait(dve, w_mm, m + 1)
                nc.vector.tensor_tensor(acc[:, lm, :], acc[:, lm, :], psW[:], ALU.add).then_inc(w_added, 1)

            def steps(g, first, last):
                for l in range(STEPS):
                    n = STEPS * g + l
                    par, s = l // 4, l % 4
                    if not (last and l == STEPS - 1):
                        row_max(n + 1, (l + 1) % STEPS)
                    wait(dve, pT_hi_done, n + 1)
                    nc.vector.tensor_tensor(pT_lo[:], psT[:].rearrange("p a b -> p (a b)")[:, 0:768], fp(pT_hi[:]),
                                            ALU.subtract).then_inc(pT_lo_done, 1)
                    if not (last and par == 1):
                        q_low(n + 5, 1 - par, s)
                        if s == 0:
                            kv_low(4 * g + 2 * par + 3, k_hi[1 - par][:], k_lo[1 - par][:])
                        if s == 1:
                            kv_low(4 * g + 2 * par + 4, v_hi[1 - par][:].rearrange("p t d -> p (t d)"),
                                   v_lo[1 - par][:].rearrange("p t d -> p (t d)"))
                    if not (last and l == STEPS - 1):
                        normalise_probs(n + 1, (l + 1) % STEPS)
                    if not (first and l < 2):
                        add_tile(n - 2, (l - 2) % STEPS)
                    wait(dve, o_hi_done, n + 1)
                    b_in, hp = s // 2, l % 2
                    nc.vector.tensor_tensor(o_lo[:, b_in, 2 * hp:2 * hp + 2, :],
                                            psO[:].rearrange("p (j q) -> p j q", j=2),
                                            fp(o_hi[:, b_in, 2 * hp:2 * hp + 2, :]), ALU.subtract).then_inc(o_lo_done, 1)
                    if last:
                        if l == 3:
                            attn_stats(0)
                        if l == 5:
                            attn_stats(1)
                            residual(0)
                        if l == 7:
                            attn_stats(2)
                            residual(1)

            groups(dve, steps)
            add_tile(NSTEP - 2, 6)
            add_tile(NSTEP - 1, 7)
            attn_stats(3)
            residual(2)
            for t in range(4):
                turned(TILES + t)
            residual(3)
            for t in range(4, TILES):
                turned(TILES + t)

            done = [0]

            def then(ins):
                done[0] += 1
                ins.then_inc(router_step, 1)
                dve.wait_ge(router_step, done[0])

            def spread(t):
                return t[:].rearrange("p (t a) -> p t a", a=1).to_broadcast([P, TILES, NE])

            dve.wait_ge(router_mm, 1)
            logits = psKV[:, 0:TILES * NE].rearrange("p (t e) -> p t e", t=TILES)
            then(nc.vector.tensor_reduce(top1[:], logits, AX_X, ALU.max))
            then(nc.vector.tensor_tensor(probs[:], logits, spread(top1), ALU.subtract))
            nc.vector.memset(comb[:, NE:NX, :], 1.0).then_inc(router_step, 1)
            done[0] += 1
            for e in range(NE):
                nc.vector.memset(rank[:, :, e:e + 1], float(NE - e)).then_inc(router_step, 1)
            done[0] += NE
            dve.wait_ge(router_exp, 1)
            then(nc.vector.tensor_reduce(tsum[:], probs[:], AX_X, ALU.add))
            then(nc.vector.reciprocal(tinv[:], tsum[:]))
            then(nc.vector.tensor_tensor(probs[:], probs[:], spread(tinv), ALU.mult))
            then(nc.vector.tensor_copy(left[:], probs[:]))
            for best, chosen in ((top1, first), (top2, second)):
                then(nc.vector.tensor_reduce(best[:], left[:], AX_X, ALU.max))
                then(nc.vector.tensor_tensor(chosen[:], left[:], spread(best), ALU.is_equal))
                then(nc.vector.tensor_tensor(chosen[:], chosen[:], rank[:], ALU.mult))
                then(nc.vector.tensor_reduce(low[:], chosen[:], AX_X, ALU.max))
                then(nc.vector.tensor_tensor(chosen[:], rank[:], spread(low), ALU.is_equal))
                then(nc.vector.scalar_tensor_tensor(out=left[:], in0=chosen[:], scalar=-2.0, in1=left[:],
                                                    op0=ALU.mult, op1=ALU.add))
            then(nc.vector.tensor_tensor(tsum[:], top1[:], top2[:], ALU.add))
            then(nc.vector.reciprocal(tinv[:], tsum[:]))
            then(nc.vector.tensor_tensor(first[:], first[:], second[:], ALU.add))
            then(nc.vector.tensor_tensor(first[:], first[:], probs[:], ALU.mult))
            then(nc.vector.tensor_tensor(comb[:, 0:NE, :].rearrange("p e t -> p t e"), first[:], spread(tinv), ALU.mult))

            def hidden(w, th):
                wait(dve, silu_done, w + 1)
                wait(dve, u_mm, w + 1)
                nc.vector.tensor_tensor(hid[th][:], silu[th][:], bank_up[th], ALU.mult).then_inc(hid_done, 1)
                wait(dve, hid_hi_done, w + 1)
                nc.vector.tensor_tensor(hid_lo[th][:], hid[th][:], fp(hid_hi[th][:]),
                                        ALU.subtract).then_inc(hid_lo_done, 1)

            def add_down(w, th, j, first):
                for i in range(4):
                    t = 4 * th + i
                    wait(dve, d_mm, 4 * w + i + 1)
                    if first:
                        nc.vector.tensor_scalar(acc2[:, t, :], bank_down[i], comb_e[:, j, t:t + 1], None,
                                                ALU.mult).then_inc(d_added, 1)
                        continue
                    wait(dve, d_added, 4 * w + i - 7)
                    nc.vector.scalar_tensor_tensor(out=acc2[:, t, :], in0=bank_down[i], scalar=comb_e[:, j, t:t + 1],
                                                   in1=acc2[:, t, :], op0=ALU.mult, op1=ALU.add).then_inc(d_added, 1)

            def pair_units(i, first):
                for j in range(2):
                    for th in range(2):
                        w = 4 * i + 2 * j + th
                        hidden(w, th)
                        if not (first and j == 0 and th == 0):
                            pj, pth = (j, 0) if th == 1 else (1 - j, 1)
                            if pth == 0:
                                wait(dve, comb_e_done, 2 * i + j + 1)
                            add_down(w - 1, pth, pj, first and w <= 2)
                        if th == 0:
                            nc.vector.tensor_copy(comb_e[:, j, :].rearrange("p (a t) -> p a t", a=1),
                                                  comb[:, bass.ds(2 * i + j, 1), :]).then_inc(comb_e_done, 1)

            pair_units(0, True)
            with dve.Fori(1, NX // 2) as i:
                pair_units(i, False)
            for p in range(4):
                if p == 2:
                    add_down(UNITS - 1, 1, 1, False)
                dve.wait_ge(d_added, 4 * UNITS - 8 + 2 * p + 2)
                stats(("y", p), acc2)
            for t in range(4, TILES):
                dve.wait_ge(normed, 2 * norm_nth["y", 0] + t + 1)
                nc.vector.tensor_tensor(acc2[:, t, :], acc2[:, t, :], x1[:, t, :], ALU.add).then_inc(y_added_dve, 1)

        @block.scalar
        def _(act):
            def copy(dst, src):
                return nc.scalar.activation(dst, src, ACT.Copy)

            def normalise(what, dst, src):
                act.wait_ge(shift_done, nth[what] + 1)
                for k in range(2):
                    t = 2 * what[1] + k
                    nc.scalar.activation(dst[:, t % dst.shape[1], :], src[:, t, :], ACT.Identity,
                                         scale=rstd[:, t:t + 1], bias=shift[:, t:t + 1]).then_inc(normed, 1)

            def turned(i):
                t = i % TILES
                act.wait_ge(turn_mm, i + 1)
                copy(xT_hi[:, :, t * P:(t + 1) * P],
                     bank_turn[i].rearrange("p (c q) -> p c q", c=CH)).then_inc(xT_hi_done, 1)

            def even_latents(j):
                act.wait_ge(lat_mm, j + 1)
                half, hp = j // 4, j % 4
                src = bank_lat[j % 3][0:64, :].rearrange("p (b t c r) -> p r c b t", b=2, t=32, c=4)
                for r in range(2):
                    dst = lat[64 * r:64 * r + 64, :, half * PAIR:(half + 1) * PAIR].rearrange(
                        "p c (b t) -> p c b t", b=2)[:, :, :, 2 * hp * 32:2 * hp * 32 + 32]
                    copy(dst, src[:, r]).then_inc(lat_even_done, 1)

            def latent_high(c):
                copy(wl_hi[:, c, :], wl_raw[:, c, :]).then_inc(wl_hi_done, 1)

            normalise(("x", 0), x_in, x_in)
            act.wait_ge(wl_landed, 16)
            latent_high(0)
            latent_high(1)
            normalise(("x", 1), x_in, x_in)
            turned(0)
            turned(1)
            latent_high(2)
            latent_high(3)
            turned(2)
            turned(3)
            normalise(("x", 2), x_in, x_in)
            normalise(("x", 3), x_in, x_in)
            for j in range(4):
                even_latents(j)
                turned(4 + j)

            def kv_high(count, dst):
                wait(act, kv_mm, count)
                copy(dst, psKV[:]).then_inc(kv_hi_done, 1)

            def q_high(count, par, h):
                wait(act, q_mm, count)
                copy(q_hi[par][:, h, :], psQ[:]).then_inc(q_hi_done, 1)

            def exponentials(n, l):
                wait(act, nmax_done, n + 1)
                for i in range(4):
                    p = s_sb[l % 2][:, i // 2, i % 2, :]
                    nc.scalar.activation(p, p, ACT.Exp, bias=nmax[:, l % 2, i:i + 1],
                                         accum_out=rsum[:, l % 2, i:i + 1]).then_inc(exp_done, 1)

            kv_high(1, k_hi[0][:])
            for h in range(HPG):
                q_high(h + 1, 0, h)
                if h == 0:
                    kv_high(2, v_hi[0][:].rearrange("p t d -> p (t d)"))
                if h == 1:
                    exponentials(0, 0)
                if h > 1:
                    even_latents(2 + h)
            even_latents(6)
            even_latents(7)

            def steps(g, first, last):
                for l in range(STEPS):
                    n = STEPS * g + l
                    par, s = l // 4, l % 4
                    wait(act, pT_mm, n + 1)
                    wait(act, o_mm, n)
                    copy(pT_hi[:], psT[:].rearrange("p a b -> p (a b)")[:, 0:768]).then_inc(pT_hi_done, 1)
                    if not (last and l == STEPS - 1):
                        exponentials(n + 1, (l + 1) % STEPS)
                    if not (last and par == 1):
                        q_high(n + 5, 1 - par, s)
                        if s == 0:
                            kv_high(4 * g + 2 * par + 3, k_hi[1 - par][:])
                        if s == 1:
                            kv_high(4 * g + 2 * par + 4, v_hi[1 - par][:].rearrange("p t d -> p (t d)"))
                    wait(act, o_mm, n + 1)
                    b_in, hp = s // 2, l % 2
                    if not (first and l < 4):
                        wait(act, w_mm, n - 2 if hp == 0 else n - 3)
                    copy(o_hi[:, b_in, 2 * hp:2 * hp + 2, :],
                         psO[:].rearrange("p (j q) -> p j q", j=2)).then_inc(o_hi_done, 1)
                    if last and l == 4:
                        normalise(("a", 0), acc, acc)
                    if last and l == 6:
                        normalise(("a", 1), acc, acc)
                        normalise(("b", 0), xn, x1)

            groups(act, steps)

            normalise(("a", 2), acc, acc)
            normalise(("b", 1), xn, x1)
            turned(TILES)
            turned(TILES + 1)
            normalise(("a", 3), acc, acc)
            turned(TILES + 2)
            turned(TILES + 3)
            normalise(("b", 2), xn, x1)
            normalise(("b", 3), xn, x1)
            for t in range(4, TILES):
                turned(TILES + t)
            act.wait_ge(router_step, 2)
            nc.scalar.activation(probs[:], probs[:], ACT.Exp).then_inc(router_exp, 1)

            def unit(w, th):
                wait(act, g_mm, w + 1)
                wait(act, hid_done, w - 1)
                nc.scalar.activation(silu[th][:], bank_gate[th], ACT.Silu).then_inc(silu_done, 1)
                wait(act, hid_done, w + 1)
                wait(act, d_mm, 4 * w - 4)
                copy(hid_hi[th][:], hid[th][:]).then_inc(hid_hi_done, 1)

            for w in range(4):
                unit(w, w % 2)
            with act.Fori(1, NX // 2) as i:
                for w in range(4):
                    unit(4 * i + w, w % 2)
            for p in range(4):
                normalise(("y", p), acc2, acc2)


def kernel(L0_attn_hidden_states, L0_attn_Wq, L0_attn_Wk_down, L0_attn_Wv_down, L0_attn_Wk_up, L0_attn_Wv_up,
           L0_attn_Wo, L0_ffn_gate_w, L0_ffn_w_gate_up, L0_ffn_w_down, L0_ffn_shared_w_gate_up,
           L0_ffn_shared_w_down):
    import numpy as _np
    import concourse.bacc as _bacc
    from concourse import mybir as _mybir
    from concourse.bass_utils import run_bass_kernel_spmd as _run

    c = _np.ascontiguousarray
    heads = NG * HPG
    w_down_k = _np.asarray(L0_attn_Wk_down).reshape(NG, 32, HID)
    w_down_v = _np.asarray(L0_attn_Wv_down).reshape(NG, 32, HID)
    lat = _np.concatenate([w_down_k, w_down_v], axis=1).reshape(HID, CH, P)
    w_gu = _np.asarray(L0_ffn_w_gate_up).reshape(NE, 2, INTER, HID)
    s_gu = _np.asarray(L0_ffn_shared_w_gate_up).reshape(2, NX - NE, INTER, HID).transpose(1, 0, 2, 3)
    gu = _np.concatenate([w_gu, s_gu], axis=0).reshape(NX, 2 * INTER, CH, P)
    s_dn = _np.asarray(L0_ffn_shared_w_down).reshape(HID, NX - NE, INTER).transpose(1, 2, 0)
    up = _np.stack([_np.asarray(L0_attn_Wk_up), _np.asarray(L0_attn_Wv_up)]).reshape(2, NG, D, 2, P)
    arrays = {
        "x": c(_np.asarray(L0_attn_hidden_states).reshape(T, HID)),
        "w_lat": c(lat.transpose(2, 1, 0).reshape(P, CH * HID)),
        "w_q": c(_np.asarray(L0_attn_Wq).reshape(heads, D, CH, P).transpose(0, 3, 2, 1).reshape(heads, P, CH * D)),
        "w_o": c(_np.asarray(L0_attn_Wo).reshape(HID, heads, D).transpose(1, 2, 0)),
        "w_kv": c(up.transpose(1, 4, 0, 3, 2).reshape(NG, P, 4 * D)),
        "w_gate": c(_np.asarray(L0_ffn_gate_w).reshape(NE, CH, P).transpose(2, 1, 0).reshape(P, CH * NE)),
        "w_gu": c(gu.transpose(0, 3, 2, 1).reshape(NX, P, CH * 2 * INTER)),
        "w_dn": c(_np.concatenate([_np.asarray(L0_ffn_w_down).transpose(0, 2, 1), s_dn], axis=0)),
    }
    nc = _bacc.Bacc("TRN2", target_bir_lowering=False, num_devices=1)
    args = [nc.dram_tensor(n, a.shape, _mybir.dt.from_np(a.dtype), kind="ExternalInput").ap()
            for n, a in arrays.items()]
    args.append(nc.dram_tensor("out", (T, HID), _mybir.dt.float32, kind="ExternalOutput").ap())
    build_program(nc, *args)
    r = _run(nc, [arrays], core_ids=[0])
    return _np.asarray(r.results[0]["out"]).reshape(B, S, HID)
```

```python
from contextlib import ExitStack

import concourse.bass as bass
from concourse import mybir

ALU = mybir.AluOpType
ACT = mybir.ActivationFunctionType
AX_X = mybir.AxisListType.X
F32 = mybir.dt.float32
F32R = mybir.dt.float32r

P = 128
EPS = 1e-5
MASKED = -1e30

B, S, HID = 4, 256, 512
NG, HPG, D = 8, 4, 128
T = B * S
TILES = T // P
CH = HID // P
PAIR = 2 * S
STEPS = 8
NSTEP = NG * STEPS
QT = (slice(0, P), slice(P, 3 * P))
SMAX = 4

NE, INTER, SHARED = 16, 128, 512
NX = NE + SHARED // INTER
HALF = 512
UNITS = 2 * NX
ROUTER_READ = NE + 3


def build_program(nc, x, w_lat, w_q, w_o, w_kv, w_gate, w_gu, w_dn, out):
    x_tiles = x.rearrange("(t p) h -> p t h", p=P)
    out_tiles = out.rearrange("(t p) h -> p t h", p=P)

    top = ExitStack()
    with top:
        def sem(name):
            return top.enter_context(nc.semaphore(name))

        def allocate(stack):
            return lambda name, shape, dt=F32: stack.enter_context(nc.sbuf_tensor(name, shape, dt))

        psS = top.enter_context(nc.psum_tensor("psS", [P, 2, 512], F32))
        psT = top.enter_context(nc.psum_tensor("psT", [P, 2, 512], F32))
        psO = top.enter_context(nc.psum_tensor("psO", [P, 512], F32))
        psQ = top.enter_context(nc.psum_tensor("psQ", [P, 512], F32))
        psW = top.enter_context(nc.psum_tensor("psW", [P, 512], F32))
        psKV = top.enter_context(nc.psum_tensor("psKV", [P, 512], F32))
        bank_gate = [psS[:, 0, :], psS[:, 1, :]]
        bank_up = [psT[:, 0, :], psT[:, 1, :]]
        bank_down = [psO[:], psQ[:], psW[:], psKV[:]]
        bank_turn = [psS[:, 0, :], psS[:, 1, :], psQ[:], psW[:]] + [psS[:, t % 2, :] for t in range(4)]
        bank_turn += [psQ[:], psKV[:], psQ[:], psKV[:], psT[:, 1, :], psQ[:], psKV[:], psQ[:]]
        bank_first_up = psS[:, 1, :]
        bank_last_up = [psT[:, 1, :], psS[:, 0, :]]
        bank_last_tile = psT[:, 0, :]
        bank_logits = psW[:]
        bank_lat = [psT[:, 0, :], psT[:, 1, :], psO[:]]

        sb = allocate(top)
        ident = sb("ident", [P, P])
        mask = sb("mask", [P, 3 * P])
        zero = sb("zero", [P, 1])
        waiter = sb("waiter", [P, 4])
        xT_hi = sb("xT_hi", [P, CH, T], F32R)
        xT_lo = sb("xT_lo", [P, CH, T], F32R)
        acc = sb("acc", [P, TILES, HID])
        bn = sb("bn", [P, TILES, 6])
        mean_var = sb("mean_var", [P, TILES, 2])
        veps = sb("veps", [P, TILES])
        neg_half = sb("neg_half", [P, 2])
        neg_mean = sb("neg_mean", [P, TILES])
        rstd = sb("rstd", [P, TILES])
        shift = sb("shift", [P, TILES])
        smax = sb("smax", [P, 2, 4])
        nmax = sb("nmax", [P, 2, 4])
        rsum = sb("rsum", [P, 2, 4])
        rinv = sb("rinv", [P, 2, 4])

        attn = ExitStack()
        early = ExitStack()
        sa = allocate(early)
        x_in = sa("x_in", [P, TILES, HID])
        wl_raw = sa("wl_raw", [P, CH, HID])
        wl_hi = sa("wl_hi", [P, CH, HID], F32R)
        wl_lo = sa("wl_lo", [P, CH, HID], F32R)
        early.close()
        sa = allocate(attn)
        o_hi = sa("o_hi", [P, 2, HPG, S], F32R)
        o_lo = sa("o_lo", [P, 2, HPG, S], F32R)
        pT_hi = sa("pT_hi", [P, 768], F32R)
        pT_lo = sa("pT_lo", [P, 768], F32R)

        def pair_of(name, shape, dt=F32R):
            return sa(f"{name}_hi", shape, dt), sa(f"{name}_lo", shape, dt)

        s_sb1 = sa("s_sb1", [P, 2, 3 * P])
        k1, v1, q1 = pair_of("k1", [P, PAIR]), pair_of("v1", [P, 4, D]), pair_of("q1", [P, HPG, 2, P])
        kf1, qf1 = sa("kf1", [P, 2, P]), sa("qf1", [P, HPG, 2, P])
        s_sb0 = sa("s_sb0", [P, 2, 3 * P])
        k0, v0, q0 = pair_of("k0", [P, PAIR]), pair_of("v0", [P, 4, D]), pair_of("q0", [P, HPG, 2, P])
        kf0, qf0 = sa("kf0", [P, 2, P]), sa("qf0", [P, HPG, 2, P])
        s_sb, k_first, q_first = [s_sb0, s_sb1], [kf0, kf1], [qf0, qf1]
        (k_hi, k_lo), (v_hi, v_lo), (q_hi, q_lo) = zip(k0, k1), zip(v0, v1), zip(q0, q1)
        lat_v = sa("lat_v", [P, 2, T])
        lat_k = acc[:, 0:4, :].rearrange("p (c t) h -> p c (t h)", c=2)
        lat_k_lo = sa("lat_k_lo", [P, 2, T], F32R)
        raw = sa("raw", [P, 4, 512])
        wkv = sa("wkv", [P, 2, 2, D])
        wq_hi = sa("wq_hi", [P, HPG, CH, D], F32R)
        wq_lo = sa("wq_lo", [P, HPG, CH, D], F32R)
        wo_hi = sa("wo_hi", [P, 2, HPG, HID], F32R)
        wo_lo = sa("wo_lo", [P, 2, HPG, HID], F32R)
        lat_k_hi = sa("lat_k_hi", [P, 2, T], F32R)
        wk_hi = sa("wk_hi", [P, 2, D], F32R)
        wk_lo = sa("wk_lo", [P, 2, D], F32R)
        attn.close()

        ffn = ExitStack()
        sf = allocate(ffn)
        acc2 = sf("acc2", [P, TILES, HID])
        silu = [sf(f"silu{i}", [P, HALF]) for i in range(2)]
        hid = [sf(f"hid{i}", [P, HALF]) for i in range(2)]
        hid_hi = [sf(f"hid_hi{i}", [P, HALF], F32R) for i in range(2)]
        hid_lo = [sf(f"hid_lo{i}", [P, HALF], F32R) for i in range(2)]
        comb = sf("comb", [P, NX, TILES])
        comb_e = sf("comb_e", [P, 2, TILES])
        sf("fill_a", [P, 2 * 256 - NX * TILES - 2 * TILES])
        gu_hi, gu_lo, dn_hi, dn_lo, gu_raw, dn_raw = {}, {}, {}, {}, {}, {}

        def cut_weights(j):
            gu_hi[j] = sf(f"gu_hi{j}", [P, CH, 256], F32R)
            gu_lo[j] = sf(f"gu_lo{j}", [P, CH, 256], F32R)
            dn_hi[j] = sf(f"dn_hi{j}", [P, HID], F32R)
            dn_lo[j] = sf(f"dn_lo{j}", [P, HID], F32R)

        cut_weights(1)
        gu_raw[1] = sf("gu_raw1", [P, CH, 256])
        dn_raw[1] = sf("dn_raw1", [P, HID])
        gu_raw[0] = sf("gu_raw0", [P, CH, 256])
        dn_raw[0] = sf("dn_raw0", [P, HID])
        cut_weights(0)
        w_g = sf("w_g", [P, CH, NE])
        w_g_cut = sf("w_g_cut", [P, CH, 2, NE], F32R)
        by_expert = sf("by_expert", [2 * NE, T])
        probs = sf("probs", [P, TILES, NE])
        left = sf("left", [P, TILES, NE])
        first = sf("first", [P, TILES, NE])
        second = sf("second", [P, TILES, NE])
        rank = sf("rank", [P, TILES, NE])
        top1 = sf("top1", [P, TILES])
        top2 = sf("top2", [P, TILES])
        low = sf("low", [P, TILES])
        tsum = sf("tsum", [P, TILES])
        tinv = sf("tinv", [P, TILES])
        sf("fill_c", [P, 16 * 256 - T - 3 * CH * NE - 5 * TILES * NE - 5 * TILES])
        xn = sf("xn", [P, 4, HID])
        sf("fill_d", [P, 2 * 256])
        x1 = sf("x1", [P, TILES, HID])
        ffn.close()

        x_in_landed = [sem(f"x_in_landed{i}") for i in range(4)]
        wl_landed = sem("wl_landed")
        raw_landed = [sem(f"raw_landed{i}") for i in range(4)]
        wkv_landed = sem("wkv_landed")
        x1_landed = [sem(f"x1_landed{i}") for i in range(4)]
        gate_landed = sem("gate_landed")
        gu_landed = [sem(f"gu_landed{i}") for i in range(2)]
        dn_landed = [sem(f"dn_landed{i}") for i in range(2)]
        out_stored = sem("out_stored")
        const_step = sem("const_step")
        consts_ready = sem("consts_ready")
        acc_zeroed = sem("acc_zeroed")
        bn_done = sem("bn_done")
        aggr_done = sem("aggr_done")
        veps_done = sem("veps_done")
        rstd_done = sem("rstd_done")
        shift_done = sem("shift_done")
        normed = sem("normed")
        normed_dve = sem("normed_dve")
        x1_added_pool = sem("x1_added_pool")
        x1_added_dve = sem("x1_added_dve")
        turn_mm = sem("turn_mm")
        xT_hi_done = sem("xT_hi_done")
        xT_lo_done = sem("xT_lo_done")
        wl_hi_done = sem("wl_hi_done")
        wl_lo_done = sem("wl_lo_done")
        wl_hi_done_pool = sem("wl_hi_done_pool")
        wl_cut_pool = sem("wl_cut_pool")
        lat_mm = sem("lat_mm")
        lat_even_done = sem("lat_even_done")
        lat_odd_done = sem("lat_odd_done")
        lat_k_hi_done = sem("lat_k_hi_done")
        lat_k_lo_done = sem("lat_k_lo_done")
        wk_hi_done = sem("wk_hi_done")
        wk_cut = sem("wk_cut")
        wq_hi_done = sem("wq_hi_done")
        wq_cut = sem("wq_cut")
        wo_hi_done = sem("wo_hi_done")
        wo_cut = sem("wo_cut")
        score_mm = sem("score_mm")
        score_max = sem("score_max")
        nmax_done = sem("nmax_done")
        exp_done = sem("exp_done")
        rinv_done = sem("rinv_done")
        prob_done = sem("prob_done")
        pT_mm = sem("pT_mm")
        pT_hi_done = sem("pT_hi_done")
        pT_lo_done = sem("pT_lo_done")
        o_mm = sem("o_mm")
        o_hi_done = sem("o_hi_done")
        o_lo_done = sem("o_lo_done")
        q_mm = sem("q_mm")
        q_hi_done = sem("q_hi_done")
        q_lo_done = sem("q_lo_done")
        kv_mm = sem("kv_mm")
        kv_hi_done = sem("kv_hi_done")
        kv_lo_done = sem("kv_lo_done")
        w_mm = sem("w_mm")
        w_added = sem("w_added")
        gate_hi_done = sem("gate_hi_done")
        gate_cut = sem("gate_cut")
        by_expert_mm = sem("by_expert_mm")
        by_expert_done = sem("by_expert_done")
        router_mm = sem("router_mm")
        router_exp = sem("router_exp")
        router_step = sem("router_step")
        gu_hi_done = sem("gu_hi_done")
        gu_cut = sem("gu_cut")
        dn_hi_done = sem("dn_hi_done")
        dn_cut = sem("dn_cut")
        g_mm = sem("g_mm")
        u_mm = sem("u_mm")
        silu_done = sem("silu_done")
        hid_done = sem("hid_done")
        hid_hi_done = sem("hid_hi_done")
        hid_lo_done = sem("hid_lo_done")
        d_mm = sem("d_mm")
        d_added = sem("d_added")
        comb_e_done = sem("comb_e_done")
        y_added_dve = sem("y_added_dve")
        y_added_pool = sem("y_added_pool")

        def fp(t):
            return t.bitcast(F32)

        def wait(eng, s, value):
            if not (isinstance(value, int) and value <= 0):
                eng.wait_ge(s, value)

        order = [("x", p) for p in range(4)]
        order += [("a", 0), ("b", 0), ("a", 1), ("b", 1), ("a", 2), ("a", 3), ("b", 2), ("b", 3)]
        order += [("y", p) for p in range(4)]
        nth = {what: i for i, what in enumerate(order)}

        def normed_count(what, k):
            i = nth[what]
            return i + 1 if i < 2 else 2 * i + k - 1

        def groups(eng, body):
            body(0, True, False)
            with eng.Fori(1, NG - 1) as g:
                body(g, False, False)
            body(NG - 1, False, True)


        block = top.enter_context(nc.Block())

        @block.sync
        def _(sp):
            for i in range(4):
                sp.dma_start(x_in[:, 2 * i:2 * i + 2, :], x_tiles[:, 2 * i:2 * i + 2, :]).then_inc(x_in_landed[i], 16)
                if i == 1:
                    sp.dma_start(wl_raw[:], w_lat.rearrange("p (c n) -> p c n", c=CH)).then_inc(wl_landed, 16)

            def pieces(g, first, last):
                if first:
                    sp.dma_start(wkv[:], w_kv[0].rearrange("p (a c d) -> p a c d", a=2, c=2)).then_inc(wkv_landed, 16)
                kinds = ((w_q, wq_cut), (w_o, wo_cut))
                turns = [(h, kind) for h in range(HPG) for kind in range(2)]
                for h, kind in sorted(turns, key=lambda turn: turn[1]) if first else turns:
                    weights, cut = kinds[kind]
                    slot = 2 * (h % 2) + kind
                    if not (first and h < 2):
                        wait(sp, cut, 4 * g + h - 1)
                    sp.dma_start(raw[:, slot, :], weights[HPG * g + h]).then_inc(raw_landed[slot], 16)
                if not first:
                    wait(sp, kv_mm, 4 * g)
                    sp.dma_start(wkv[:], w_kv[g].rearrange("p (a c d) -> p a c d", a=2, c=2)).then_inc(wkv_landed, 16)

            groups(sp, pieces)

            for i in range(4):
                sp.wait_ge(q_mm, NSTEP if i else NSTEP - 2)
                sp.dma_start(x1[:, 2 * i:2 * i + 2, :], x_tiles[:, 2 * i:2 * i + 2, :]).then_inc(x1_landed[i], 16)
            sp.wait_ge(kv_mm, 4 * NG)
            sp.dma_start(w_g[:], w_gate.rearrange("p (c e) -> p c e", c=CH)).then_inc(gate_landed, 16)
            sp.wait_ge(o_mm, NSTEP - 4)

            def expert(e, j, first):
                if not first:
                    wait(sp, gu_cut, e - 1)
                sp.dma_start(gu_raw[j][:], w_gu[e].rearrange("p (c n) -> p c n", c=CH)).then_inc(gu_landed[j], 16)
                if not first:
                    wait(sp, dn_cut, e - 1)
                sp.dma_start(dn_raw[j][:], w_dn[e]).then_inc(dn_landed[j], 16)

            expert(0, 0, True)
            sp.wait_ge(pT_mm, NSTEP - 1)
            expert(1, 1, True)
            with sp.Fori(1, NX // 2) as pair:
                expert(2 * pair, 0, False)
                expert(2 * pair + 1, 1, False)

            for t in range(TILES):
                if t < 4:
                    sp.wait_ge(y_added_pool, t + 1)
                else:
                    sp.wait_ge(y_added_dve, t - 3)
                sp.dma_start(out_tiles[:, t, :], acc2[:, t, :]).then_inc(out_stored, 16)
            sp.wait_ge(out_stored, 16 * TILES)

        @block.gpsimd
        def _(pool):
            nc.gpsimd.memset(ident[:], 0.0).then_inc(const_step, 1)
            nc.gpsimd.memset(neg_half[:], -0.5).then_inc(const_step, 1)
            nc.gpsimd.memset(zero[:], 0.0).then_inc(const_step, 1)
            pool.wait_ge(const_step, 3)
            nc.gpsimd.affine_select(out=ident[:], in_=ident[:], compare_op=ALU.not_equal, fill=1.0, base=0,
                                    pattern=[[-1, P]], channel_multiplier=1).then_inc(consts_ready, 1)

            def scale_and_shift(what):
                i, t = nth[what], 2 * what[1]
                pool.wait_ge(veps_done, 2 * i + 2)
                nc.gpsimd.tensor_tensor(rstd[:, t:t + 2], veps[:, t:t + 2], neg_half[:], ALU.pow).then_inc(rstd_done, 1)
                pool.wait_ge(rstd_done, i + 1)
                nc.gpsimd.tensor_tensor(shift[:, t:t + 2], neg_mean[:, t:t + 2], rstd[:, t:t + 2],
                                        ALU.mult).then_inc(shift_done, 1)

            def round_to(dst, src):
                z = zero[:]
                for n in src.shape[2:]:
                    z = z.rearrange("p (a b) -> p a b", b=1) if len(z.shape) < len(src.shape) else z
                return nc.gpsimd.tensor_tensor(dst, src, z.to_broadcast(list(src.shape)), ALU.add)

            scale_and_shift(("x", 0))
            scale_and_shift(("x", 1))
            pool.wait_ge(wl_landed, 16)
            for i, c in enumerate((2, 3)):
                round_to(wl_hi[:, c, :], wl_raw[:, c, :]).then_inc(wl_hi_done_pool, 1)
                pool.wait_ge(wl_hi_done_pool, i + 1)
                nc.gpsimd.tensor_tensor(wl_lo[:, c, :], wl_raw[:, c, :], fp(wl_hi[:, c, :]),
                                        ALU.subtract).then_inc(wl_cut_pool, 1)
            scale_and_shift(("x", 2))
            scale_and_shift(("x", 3))

            def cut_queries(g, h, first):
                if not first:
                    wait(pool, q_mm, 8 * g + h - 3)
                wait(pool, raw_landed[2 * (h % 2)], 32 * g + 16 * (h // 2) + 16)
                src = raw[:, 2 * (h % 2), :].rearrange("p (c d) -> p c d", c=CH)
                round_to(wq_hi[:, h], src).then_inc(wq_hi_done, 1)
                wait(pool, wq_hi_done, 4 * g + h + 1)
                nc.gpsimd.tensor_tensor(wq_lo[:, h], src, fp(wq_hi[:, h]), ALU.subtract).then_inc(wq_cut, 1)

            def cut_keys(g, first):
                wait(pool, wkv_landed, 16 * g + 16)
                if not first:
                    wait(pool, kv_mm, 4 * g)
                round_to(wk_hi[:], wkv[:, 0]).then_inc(wk_hi_done, 1)
                wait(pool, wk_hi_done, g + 1)
                nc.gpsimd.tensor_tensor(wk_lo[:], wkv[:, 0], fp(wk_hi[:]), ALU.subtract).then_inc(wk_cut, 1)

            def cut_outputs(g, h, first):
                if first:
                    pool.wait_ge(lat_mm, 8)
                elif h == 0:
                    wait(pool, w_mm, 8 * g - 8)
                wait(pool, raw_landed[2 * (h % 2) + 1], 32 * g + 16 * (h // 2) + 16)
                src = raw[:, 2 * (h % 2) + 1, :]
                slot = g % 2
                round_to(wo_hi[:, slot, h], src).then_inc(wo_hi_done, 1)
                wait(pool, wo_hi_done, 4 * g + h + 1)
                nc.gpsimd.tensor_tensor(wo_lo[:, slot, h], src, fp(wo_hi[:, slot, h]),
                                        ALU.subtract).then_inc(wo_cut, 1)

            def cut(g, first, last):
                if not first:
                    for h in range(HPG):
                        if h == 2:
                            cut_keys(g, False)
                        cut_queries(g, h, False)
                        cut_outputs(g, h, False)
                    return
                cut_queries(0, 0, True)
                cut_keys(0, True)
                nc.gpsimd.memset(mask[:], 0.0).then_inc(const_step, 1)
                pool.wait_ge(const_step, 4)
                for at in (0, 2 * P):
                    nc.gpsimd.affine_select(out=mask[:, at:at + P], in_=mask[:, at:at + P], compare_op=ALU.is_ge,
                                            fill=MASKED, base=0, pattern=[[-1, P]],
                                            channel_multiplier=1).then_inc(consts_ready, 1)
                for h in range(1, HPG):
                    cut_queries(0, h, True)
                nc.gpsimd.memset(acc[:, TILES - 2:, :], 0.0).then_inc(acc_zeroed, 1)
                for h in range(HPG):
                    cut_outputs(0, h, True)

            groups(pool, cut)

            def residual(p):
                pool.wait_ge(x1_landed[p], 16)
                for k in range(2):
                    t = 2 * p + k
                    pool.wait_ge(normed, normed_count(("a", p), k))
                    nc.gpsimd.tensor_tensor(x1[:, t, :], x1[:, t, :], acc[:, t, :], ALU.add).then_inc(x1_added_pool, 1)

            def cut_gate_up(i, j, first):
                e = 2 * i + j
                wait(pool, gu_landed[j], 16 * i + 16)
                if not first:
                    wait(pool, u_mm, 2 * e - 1)
                round_to(gu_hi[j][:], gu_raw[j][:]).then_inc(gu_hi_done, 1)
                wait(pool, gu_hi_done, e + 1)
                nc.gpsimd.tensor_tensor(gu_lo[j][:], gu_raw[j][:], fp(gu_hi[j][:]), ALU.subtract).then_inc(gu_cut, 1)

            def cut_down(i, j, first):
                e = 2 * i + j
                wait(pool, dn_landed[j], 16 * i + 16)
                if not first:
                    wait(pool, d_mm, 8 * e - 8)
                round_to(dn_hi[j][:], dn_raw[j][:]).then_inc(dn_hi_done, 1)
                wait(pool, dn_hi_done, e + 1)
                nc.gpsimd.tensor_tensor(dn_lo[j][:], dn_raw[j][:], fp(dn_hi[j][:]), ALU.subtract).then_inc(dn_cut, 1)

            scale_and_shift(("a", 0))
            residual(0)
            scale_and_shift(("b", 0))
            pool.wait_ge(o_mm, NSTEP - 4)
            cut_gate_up(0, 0, True)
            scale_and_shift(("a", 1))
            residual(1)
            pool.wait_ge(gate_landed, 16)
            round_to(w_g_cut[:, :, 0, :], w_g[:]).then_inc(gate_hi_done, 1)
            pool.wait_ge(gate_hi_done, 1)
            nc.gpsimd.tensor_tensor(w_g_cut[:, :, 1, :], w_g[:], fp(w_g_cut[:, :, 0, :]),
                                    ALU.subtract).then_inc(gate_cut, 1)
            scale_and_shift(("b", 1))
            scale_and_shift(("a", 2))
            pool.wait_ge(score_mm, 2 * NSTEP)
            cut_gate_up(0, 1, True)
            for what in (("a", 3), ("b", 2), ("b", 3)):
                scale_and_shift(what)
            cut_down(0, 0, True)
            cut_down(0, 1, True)
            with pool.Fori(1, NX // 2) as pair:
                for j in range(2):
                    cut_gate_up(pair, j, False)
                    cut_down(pair, j, False)

            for p in range(4):
                scale_and_shift(("y", p))
                for t in ((), (0, 1, 2, 3), (), ())[p]:
                    pool.wait_ge(normed, normed_count(("y", t // 2), t % 2))
                    nc.gpsimd.tensor_tensor(acc2[:, t, :], acc2[:, t, :], x1[:, t, :],
                                            ALU.add).then_inc(y_added_pool, 1)

        @block.tensor
        def _(pe):
            def three(dst, hi_l, lo_l, hi_r, lo_r, start, stop):
                nc.tensor.matmul(dst, hi_l, hi_r, start=start, stop=False)
                nc.tensor.matmul(dst, hi_l, lo_r, start=False, stop=False)
                return nc.tensor.matmul(dst, lo_l, hi_r, start=False, stop=stop)

            def turn(i, src):
                for c in range(CH):
                    mm = nc.tensor.transpose(bank_turn[i][:, c * P:(c + 1) * P], src[:, c * P:(c + 1) * P], ident[:])
                mm.then_inc(turn_mm, 1)

            pe.wait_ge(consts_ready, 1)
            for t in range(4):
                pe.wait_ge(normed_dve if t % 2 else normed, t // 2 + 1)
                turn(t, x_in[:, t, :])

            def latents(j):
                half, hp = j // 4, j % 4
                pe.wait_ge(xT_lo_done, 4 * half + 4)
                wait(pe, lat_even_done, 4 * (j - 2))
                wait(pe, lat_odd_done, 4 * (j - 2))
                rows = slice(hp * P, (hp + 1) * P)
                cols = slice(half * PAIR, (half + 1) * PAIR)
                for c in range(CH):
                    if j == 0:
                        pe.wait_ge(wl_lo_done if c < 2 else wl_cut_pool, c % 2 + 1)
                    mm = three(bank_lat[j % 3], wl_hi[:, c, rows], wl_lo[:, c, rows],
                               xT_hi[:, c, cols], xT_lo[:, c, cols], c == 0, c == CH - 1)
                mm.then_inc(lat_mm, 1)

            for j in range(4):
                latents(j)
                t = 4 + j
                pe.wait_ge(normed, normed_count(("x", t // 2), t % 2))
                wait(pe, xT_lo_done, t - 1)
                turn(t, x_in[:, t, :])

            def keys(u, par):
                cols = slice(par * PAIR, (par + 1) * PAIR)
                for c in range(2):
                    mm = three(psKV[:], wk_hi[:, c, :], wk_lo[:, c, :], lat_k_hi[:, c, cols], lat_k_lo[:, c, cols],
                               c == 0, c == 1)
                mm.then_inc(kv_mm, 1)

            def values(u, par):
                for t in range(4):
                    for c in range(2):
                        mm = nc.tensor.matmul(psKV[:, t * D:(t + 1) * D],
                                              lat_v[:, c, par * PAIR + t * P:par * PAIR + (t + 1) * P],
                                              wkv[:, 1, c, :], start=c == 0, stop=c == 1)
                mm.then_inc(kv_mm, 1)

            def queries(h, par):
                for c in range(CH):
                    mm = three(psQ[:], wq_hi[:, h, c, :], wq_lo[:, h, c, :],
                               xT_hi[:, c, par * PAIR:(par + 1) * PAIR], xT_lo[:, c, par * PAIR:(par + 1) * PAIR],
                               c == 0, c == CH - 1)
                mm.then_inc(q_mm, 1)

            def scores(n, l):
                par, b_in, hp = l // 4, l % 4 // 2, l % 2
                u_done = 4 * (n // 4) if isinstance(n, int) else n - l % 4
                wait(pe, kv_lo_done, 2 * (n // 4) + 1 if isinstance(n, int) else (n - l % 4) // 2 + 1)
                wait(pe, q_lo_done, u_done + 2 * hp + 2)
                for j in range(2):
                    h = 2 * hp + j
                    wait(pe, score_max, SMAX * n - 2 + 2 * j)
                    nc.tensor.matmul(psS[:, j, 0:P], q_first[par][:, h, b_in, :], k_first[par][:, b_in, :],
                                     start=True, stop=True)
                    ks = slice(b_in * S, (b_in + 1) * S)
                    mm = three(psS[:, j, P:3 * P], q_hi[par][:, h, b_in, :], q_lo[par][:, h, b_in, :],
                               k_hi[par][:, ks], k_lo[par][:, ks], True, True)
                    mm.then_inc(score_mm, 1)

            def turn_probs(n, l):
                wait(pe, prob_done, 4 * n + 4)
                wait(pe, pT_lo_done, n)
                p_sb = s_sb[l % 2]
                for j in range(2):
                    for qt in range(2):
                        nc.tensor.transpose(psT[:, 0, j * 256 + qt * P:j * 256 + (qt + 1) * P],
                                            p_sb[:, j, qt * P:(qt + 1) * P], ident[:])
                    mm = nc.tensor.transpose(psT[:, 1, j * P:(j + 1) * P], p_sb[:, j, 2 * P:3 * P], ident[:])
                mm.then_inc(pT_mm, 1)

            def attend(n, l):
                par, b_in = l // 4, l % 4 // 2
                wait(pe, pT_lo_done, n + 1)
                if l % 4 == 0:
                    wait(pe, kv_lo_done, n // 2 + 2)
                wait(pe, o_lo_done, n)
                v0, v1 = 2 * b_in, 2 * b_in + 1
                three(psO[:], v_hi[par][:, v0, :], v_lo[par][:, v0, :], pT_hi[:, 0:512], pT_lo[:, 0:512], True, False)
                late = psO[:].rearrange("p (j q) -> p j q", j=2)[:, :, P:2 * P]
                mm = three(late, v_hi[par][:, v1, :], v_lo[par][:, v1, :],
                           pT_hi[:, 512:768].rearrange("p (j q) -> p j q", j=2),
                           pT_lo[:, 512:768].rearrange("p (j q) -> p j q", j=2), False, True)
                mm.then_inc(o_mm, 1)

            def project(m, lm, slot, bank=None):
                b_in, tt = lm % 4 // 2, lm % 2
                wait(pe, o_lo_done, m - tt + 2)
                if bank is None:
                    bank = psW[:]
                    wait(pe, w_added, m)
                for h in range(HPG):
                    at = slice(tt * P, (tt + 1) * P)
                    mm = three(bank, o_hi[:, b_in, h, at], o_lo[:, b_in, h, at],
                               wo_hi[:, slot, h, :], wo_lo[:, slot, h, :], h == 0, h == HPG - 1)
                mm.then_inc(w_mm, 1)

            for h in range(HPG):
                pe.wait_ge(wq_cut, h + 1)
                wait(pe, q_lo_done, h)
                queries(h, 0)
                if h == 1:
                    pe.wait_ge(kv_lo_done, 1)
                    values(0, 0)
                latents(4 + h)
                if h == 0:
                    pe.wait_ge(wk_cut, 1)
                    pe.wait_ge(lat_k_lo_done, 1)
                    keys(0, 0)
                if h == 1:
                    scores(0, 0)

            def gate_up_tiles(part, bank, p, j=0):
                cols, at = slice(p * 2 * P, (p + 1) * 2 * P), slice(p % 2 * 2 * P, (p % 2 + 1) * 2 * P)
                weights = slice(part * P, (part + 1) * P)
                for c in range(CH):
                    mm = three(bank[:, at], gu_hi[j][:, c, weights], gu_lo[j][:, c, weights],
                               xT_hi[:, c, cols], xT_lo[:, c, cols], c == 0, c == CH - 1)
                return mm

            def turn_x1(t):
                pe.wait_ge(normed, normed_count(("b", t // 2), t % 2))
                bank_read, count = ((q_lo_done, NSTEP), (kv_lo_done, 4 * NG), (xT_lo_done, TILES + 1),
                                    (xT_lo_done, TILES + 2), (pT_lo_done, NSTEP), (xT_lo_done, TILES + 3),
                                    (xT_lo_done, TILES + 4), (xT_lo_done, TILES + 6))[t]
                pe.wait_ge(bank_read, count)
                turn(TILES + t, xn[:, t % 4, :])

            def steps(g, first, last):
                for l in range(STEPS):
                    n = STEPS * g + l
                    par, s = l // 4, l % 4
                    if not (last and l == STEPS - 1):
                        scores(n + 1, (l + 1) % STEPS)
                    if first and l == 0:
                        pe.wait_ge(lat_even_done, 32)
                        pe.wait_ge(lat_odd_done, 32)
                    turn_probs(n, l)
                    if not (last and par == 1):
                        wait(pe, wq_cut, 4 * g + s + 1 + 4 * par)
                        wait(pe, q_lo_done, n + 4)
                        queries(s, 1 - par)
                        if first and l == 0:
                            attend(n, l)
                        if s < 2:
                            if s == 0 and par == 1:
                                wait(pe, wk_cut, g + 2)
                            if s == 1 and par == 1:
                                wait(pe, wkv_landed, 16 * g + 32)
                            if s == 0 and first and par == 0:
                                wait(pe, lat_k_lo_done, 2)
                            wait(pe, kv_lo_done, (4 * g + 2 * par + 2) + s)
                            (keys if s == 0 else values)(None, 1 - par)
                    if not (first and l < 2):
                        lm = (l - 2) % STEPS
                        if l == 2:
                            wait(pe, wo_cut, 4 * g + 4)
                        project(n - 2, lm, (g if l >= 2 else g + 1) % 2)
                    if last and l == 6:
                        turn_x1(0)
                        turn_x1(1)
                    if last and l == 7:
                        pe.wait_ge(score_max, SMAX * NSTEP)
                        pe.wait_ge(xT_lo_done, TILES + 2)
                        pe.wait_ge(gu_cut, 1)
                        gate_up_tiles(0, bank_gate[0], 0)
                    if not (first and l == 0):
                        attend(n, l)

            groups(pe, steps)

            gate_up_tiles(1, bank_first_up, 0)
            project(NSTEP - 2, 6, (NG - 1) % 2)
            turn_x1(2)
            turn_x1(3)
            pe.wait_ge(pT_lo_done, NSTEP)
            project(NSTEP - 1, 7, (NG - 1) % 2, bank_last_tile)

            def logits_by_expert(th):
                if th == 0:
                    pe.wait_ge(gate_cut, 1)
                    pe.wait_ge(o_lo_done, NSTEP)
                else:
                    pe.wait_ge(by_expert_done, th)
                cols = slice(th * HALF, (th + 1) * HALF)
                for c in range(CH):
                    weights = w_g_cut[:, c, :, :].rearrange("p a e -> p (a e)")
                    nc.tensor.matmul(psO[0:2 * NE, :], weights, xT_hi[:, c, cols], start=c == 0, stop=False)
                    mm = nc.tensor.matmul(psO[0:2 * NE, :], weights, xT_lo[:, c, cols], start=False, stop=c == CH - 1)
                mm.then_inc(by_expert_mm, 1)

            def logits_by_token(th):
                pe.wait_ge(by_expert_done, th + 1)
                if th == 0:
                    pe.wait_ge(w_added, NSTEP)
                for t in range(4 * th, 4 * th + 4):
                    for part in range(2):
                        mm = nc.tensor.matmul(bank_logits[:, t * NE:(t + 1) * NE], by_expert[:, t * P:(t + 1) * P],
                                              ident[0:2 * NE, part * NE:(part + 1) * NE],
                                              start=part == 0, stop=part == 1)
                mm.then_inc(router_mm, 1)

            def gate(w, e, th, j):
                if th == 0:
                    wait(pe, gu_cut, e + 1)
                wait(pe, silu_done, w - 1)
                cols = slice(th * HALF, (th + 1) * HALF)
                for c in range(CH):
                    mm = three(bank_gate[th], gu_hi[j][:, c, 0:P], gu_lo[j][:, c, 0:P],
                               xT_hi[:, c, cols], xT_lo[:, c, cols], c == 0, c == CH - 1)
                mm.then_inc(g_mm, 1)

            def up(w, th, j):
                wait(pe, hid_done, w - 1)
                cols = slice(th * HALF, (th + 1) * HALF)
                for c in range(CH):
                    mm = three(bank_up[th], gu_hi[j][:, c, P:2 * P], gu_lo[j][:, c, P:2 * P],
                               xT_hi[:, c, cols], xT_lo[:, c, cols], c == 0, c == CH - 1)
                mm.then_inc(u_mm, 1)

            def down(w, e, th, j, first):
                wait(pe, hid_lo_done, w + 1)
                if th == 0:
                    wait(pe, dn_cut, e + 1)
                for i in range(4):
                    if not first:
                        wait(pe, d_added, 4 * w + i - 3)
                    elif w == 0 and i == 0:
                        pe.wait_ge(by_expert_done, 2)
                    elif w == 0 and i == 2:
                        pe.wait_ge(router_step, ROUTER_READ)
                    if isinstance(w, int) and w == UNITS - 1 and i == 2:
                        pe.wait_ge(hid_lo_done, UNITS + 1)
                    at = slice(i * P, (i + 1) * P)
                    three(bank_down[i], hid_hi[th][:, at], hid_lo[th][:, at], dn_hi[j][:], dn_lo[j][:],
                          True, True).then_inc(d_mm, 1)

            pe.wait_ge(xT_lo_done, TILES + 4)
            gate_up_tiles(0, bank_gate[0], 1).then_inc(g_mm, 1)
            gate_up_tiles(1, bank_first_up, 1).then_inc(u_mm, 1)
            logits_by_expert(0)
            gate(2, 1, 0, 1)
            logits_by_token(0)
            turn_x1(4)
            turn_x1(5)
            up(2, 0, 1)
            turn_x1(6)
            turn_x1(7)
            pe.wait_ge(hid_done, 1)
            pe.wait_ge(xT_lo_done, TILES + 6)
            gate_up_tiles(0, bank_gate[1], 2)
            gate_up_tiles(1, bank_up[1], 2)
            pe.wait_ge(xT_lo_done, 2 * TILES)
            logits_by_expert(1)
            gate_up_tiles(0, bank_gate[1], 3).then_inc(g_mm, 1)
            logits_by_token(1)
            gate_up_tiles(1, bank_up[1], 3).then_inc(u_mm, 1)

            def pair_units(i, first, last):
                for j in range(2):
                    for th in range(2):
                        w = 4 * i + 2 * j + th
                        if last and w == UNITS - 1:
                            down(w - 1, NX - 1, 0, 1, False)
                        if first and w == 2:
                            gate(3, 1, 1, 1)
                            up(3, 1, 1)
                        elif not first:
                            gate(w, 2 * i + j, th, j)
                            if last and w == UNITS - 1:
                                pe.wait_ge(hid_done, w - 1)
                                for half in range(2):
                                    wait(pe, silu_done, w)
                                    gate_up_tiles(1, bank_last_up[half], 2 + half, 1).then_inc(u_mm, 1)
                            else:
                                up(w, th, j)
                        if last and w == UNITS - 1:
                            down(w, NX - 1, 1, 1, False)
                        elif not (first and j == 0 and th == 0):
                            pj, pth = (j, 0) if th == 1 else (1 - j, 1)
                            down(w - 1, 2 * i + j - (1 - th), pth, pj, first and j == 0)

            pair_units(0, True, False)
            with pe.Fori(1, NX // 2 - 1) as i:
                pair_units(i, False, False)
            pair_units(NX // 2 - 1, False, True)

        @block.vector
        def _(dve):
            def stats(what, src):
                i, t = nth[what], 2 * what[1]
                for k in range(2):
                    nc.vector.bn_stats(bn[:, t + k, :], src[:, t + k, :]).then_inc(bn_done, 1)
                for k in range(2):
                    dve.wait_ge(bn_done, 2 * i + k + 1)
                    nc.vector.bn_aggr(mean_var[:, t + k, :], bn[:, t + k, :]).then_inc(aggr_done, 1)
                dve.wait_ge(aggr_done, 2 * i + 2)
                nc.vector.tensor_scalar(veps[:, t:t + 2], mean_var[:, t:t + 2, 1], EPS, None,
                                        ALU.add).then_inc(veps_done, 1)
                nc.vector.tensor_scalar(neg_mean[:, t:t + 2], mean_var[:, t:t + 2, 0], -1.0, None,
                                        ALU.mult).then_inc(veps_done, 1)

            def turned(i):
                t = i % TILES
                dve.wait_ge(xT_hi_done, i + 1)
                nc.vector.tensor_tensor(xT_lo[:, :, t * P:(t + 1) * P],
                                        bank_turn[i].rearrange("p (c q) -> p c q", c=CH),
                                        fp(xT_hi[:, :, t * P:(t + 1) * P]), ALU.subtract).then_inc(xT_lo_done, 1)

            def latent_low(c):
                dve.wait_ge(wl_hi_done, c + 1)
                nc.vector.tensor_tensor(wl_lo[:, c, :], wl_raw[:, c, :], fp(wl_hi[:, c, :]),
                                        ALU.subtract).then_inc(wl_lo_done, 1)

            def x_stats(p):
                dve.wait_ge(x_in_landed[p], 16)
                stats(("x", p), x_in)

            def normalise_second(p):
                dve.wait_ge(shift_done, p + 1)
                t = 2 * p + 1
                nc.vector.tensor_scalar(x_in[:, t, :], x_in[:, t, :], rstd[:, t:t + 1], shift[:, t:t + 1],
                                        ALU.mult, ALU.add).then_inc(normed_dve, 1)

            x_stats(0)
            x_stats(1)
            normalise_second(0)
            normalise_second(1)
            latent_low(0)
            turned(0)
            turned(1)
            turned(2)
            turned(3)
            latent_low(1)
            x_stats(2)
            x_stats(3)

            def latents(j, e, copy):
                half, hp = j // 4, j % 4
                src = bank_lat[j % 3][64 * e:64 * e + 64, :].rearrange("p (b t c r) -> p r c b t", b=2, t=32, c=4)
                for r in range(2):
                    for i, part in enumerate((lat_k, lat_v)):
                        dst = part[64 * r:64 * r + 64, :, half * PAIR:(half + 1) * PAIR].rearrange(
                            "p c (b t) -> p c b t", b=2)[:, :, :, (2 * hp + e) * 32:(2 * hp + e) * 32 + 32]
                        copy(dst, src[:, r, 2 * i:2 * i + 2])

            def odd_latents(j):
                dve.wait_ge(lat_mm, j + 1)
                latents(j, 1, lambda d, s: nc.vector.tensor_copy(d, s).then_inc(lat_odd_done, 1))

            def keys_low(half):
                dve.wait_ge(lat_k_hi_done, half + 1)
                cols = slice(half * PAIR, (half + 1) * PAIR)
                nc.vector.tensor_tensor(lat_k_lo[:, :, cols], lat_k[:, :, cols], fp(lat_k_hi[:, :, cols]),
                                        ALU.subtract).then_inc(lat_k_lo_done, 1)

            for j in range(4):
                odd_latents(j)
                turned(4 + j)
            keys_low(0)

            def low_part(count_sem, count, dst_lo, src, dst_hi, done):
                wait(dve, count_sem, count)
                nc.vector.tensor_tensor(dst_lo, src, fp(dst_hi), ALU.subtract).then_inc(done, 1)

            def k_low(count, par):
                low_part(kv_hi_done, count, k_lo[par][:], psKV[:], k_hi[par][:], kv_lo_done)

            def v_low(count, par):
                low_part(kv_hi_done, count, v_lo[par][:].rearrange("p t d -> p (t d)"), psKV[:],
                         v_hi[par][:].rearrange("p t d -> p (t d)"), kv_lo_done)

            def q_low(count, par, h):
                src = psQ[:].rearrange("p (b t q) -> p b t q", b=2, t=2)[:, :, 1, :]
                low_part(q_hi_done, count, q_lo[par][:, h], src, q_hi[par][:, h], q_lo_done)

            def row_max(n, l):
                for j in range(2):
                    wait(dve, score_mm, 2 * n + j + 1)
                    if j == 0:
                        wait(dve, pT_mm, n - 1)
                    nc.vector.memset(waiter[:, 2 * (l % 2) + j:2 * (l % 2) + j + 1], 0.0)
                    for qt, ks in enumerate((slice(0, P), slice(P, 3 * P))):
                        nc.vector.tensor_tensor_reduce(
                            out=s_sb[l % 2][:, j, ks], in0=psS[:, j, ks], in1=mask[:, ks],
                            scale=float(D) ** -0.5, scalar=-3e38, op0=ALU.add, op1=ALU.max,
                            accum_out=smax[:, l % 2, 2 * j + qt:2 * j + qt + 1]).then_inc(score_max, 1)
                wait(dve, score_max, SMAX * n + SMAX)
                nc.vector.tensor_scalar(nmax[:, l % 2, :], smax[:, l % 2, :], -1.0, None,
                                        ALU.mult).then_inc(nmax_done, 1)

            def normalise_probs(n, l):
                wait(dve, exp_done, 4 * n + 4)
                nc.vector.reciprocal(rinv[:, l % 2, :], rsum[:, l % 2, :]).then_inc(rinv_done, 1)
                wait(dve, rinv_done, n + 1)
                for i in range(4):
                    p = s_sb[l % 2][:, i // 2, QT[i % 2]]
                    nc.vector.tensor_scalar(p, p, rinv[:, l % 2, i:i + 1], None, ALU.mult).then_inc(prob_done, 1)

            dve.wait_ge(consts_ready, 3)
            for h in range(HPG):
                q_low(h + 1, 0, h)
                if h == 1:
                    v_low(2, 0)
                odd_latents(4 + h)
                if h == 0:
                    k_low(1, 0)
                if h == 1:
                    row_max(0, 0)
                if h == 2:
                    normalise_probs(0, 0)
            dve.wait_ge(acc_zeroed, 1)

            def attn_stats(p):
                dve.wait_ge(w_added, NSTEP - 8 + 2 * p + 2)
                stats(("a", p), acc)

            def residual(p):
                dve.wait_ge(x1_landed[p], 16)
                for k in range(2):
                    t = 2 * p + k
                    dve.wait_ge(normed, normed_count(("a", p), k))
                    nc.vector.tensor_tensor(x1[:, t, :], x1[:, t, :], acc[:, t, :], ALU.add).then_inc(x1_added_dve, 1)

            def x1_stats(p):
                if p < 2:
                    dve.wait_ge(x1_added_pool, 2 * p + 2)
                else:
                    dve.wait_ge(x1_added_dve, 2 * p - 2)
                stats(("b", p), x1)

            def add_tile(m, lm, bank=None, first=False):
                wait(dve, w_mm, m + 1)
                if first:
                    nc.vector.tensor_copy(acc[:, lm, :], psW[:]).then_inc(w_added, 1)
                    return
                nc.vector.tensor_tensor(acc[:, lm, :], acc[:, lm, :], psW[:] if bank is None else bank,
                                        ALU.add).then_inc(w_added, 1)

            def steps(g, first, last):
                for l in range(STEPS):
                    n = STEPS * g + l
                    par, s = l // 4, l % 4
                    if not (last and l == STEPS - 1):
                        row_max(n + 1, (l + 1) % STEPS)
                    wait(dve, pT_hi_done, n + 1)
                    nc.vector.tensor_tensor(pT_lo[:], psT[:].rearrange("p a b -> p (a b)")[:, 0:768], fp(pT_hi[:]),
                                            ALU.subtract).then_inc(pT_lo_done, 1)
                    if first and l == 0:
                        keys_low(1)
                    if not (last and par == 1):
                        q_low(n + 5, 1 - par, s)
                    if last:
                        if l == 4:
                            attn_stats(0)
                        if l == 5:
                            x1_stats(0)
                        if l == 6:
                            attn_stats(1)
                    if not (last and l == STEPS - 1):
                        normalise_probs(n + 1, (l + 1) % STEPS)
                    if not (last and par == 1):
                        if s == 0:
                            k_low(4 * g + 2 * par + 3, 1 - par)
                        if s == 1:
                            v_low(4 * g + 2 * par + 4, 1 - par)
                    if not (first and l < 2):
                        add_tile(n - 2, (l - 2) % STEPS, first=first)
                    if last and l == 7:
                        x1_stats(1)
                    wait(dve, o_hi_done, n + 1)
                    b_in, hp = s // 2, l % 2
                    heads = slice(2 * hp, 2 * hp + 2)
                    nc.vector.tensor_tensor(o_lo[:, b_in, heads, :], psO[:].rearrange("p (j q) -> p j q", j=2),
                                            fp(o_hi[:, b_in, heads, :]), ALU.subtract).then_inc(o_lo_done, 1)
                    if last and l == 6:
                        turned(TILES)
                        turned(TILES + 1)

            groups(dve, steps)
            attn_stats(2)
            add_tile(NSTEP - 2, 6)
            residual(2)
            turned(TILES + 2)
            turned(TILES + 3)
            add_tile(NSTEP - 1, 7, bank_last_tile)
            attn_stats(3)
            x1_stats(2)

            def hidden(w, th, bank):
                wait(dve, silu_done, w + 1)
                wait(dve, u_mm, 3 if isinstance(w, int) and w == 1 else w + 1)
                nc.vector.tensor_tensor(hid[th][:], silu[th][:], bank, ALU.mult).then_inc(hid_done, 1)

            def hidden_low(w, th):
                wait(dve, hid_hi_done, w + 1)
                nc.vector.tensor_tensor(hid_lo[th][:], hid[th][:], fp(hid_hi[th][:]),
                                        ALU.subtract).then_inc(hid_lo_done, 1)

            hidden(0, 0, bank_first_up)
            residual(3)
            x1_stats(3)
            hidden_low(0, 0)
            nc.vector.memset(comb[:, NE:NX, :], 1.0).then_inc(router_step, 1)
            for e in range(NE):
                nc.vector.memset(rank[:, :, e:e + 1], float(NE - e)).then_inc(router_step, 1)
            for t in range(4, TILES):
                turned(TILES + t)

            done = [NE + 1]

            def then(ins):
                done[0] += 1
                ins.then_inc(router_step, 1)
                dve.wait_ge(router_step, done[0])

            def spread(t):
                return t[:].rearrange("p (t a) -> p t a", a=1).to_broadcast([P, TILES, NE])

            dve.wait_ge(router_mm, 2)
            logits = bank_logits[:, 0:TILES * NE].rearrange("p (t e) -> p t e", t=TILES)
            then(nc.vector.tensor_reduce(top1[:], logits, AX_X, ALU.max))
            then(nc.vector.tensor_tensor(probs[:], logits, spread(top1), ALU.subtract))
            hidden(1, 1, bank_up[1])
            dve.wait_ge(router_exp, 1)
            then(nc.vector.tensor_reduce(tsum[:], probs[:], AX_X, ALU.add))
            then(nc.vector.reciprocal(tinv[:], tsum[:]))
            then(nc.vector.tensor_tensor(probs[:], probs[:], spread(tinv), ALU.mult))
            for best, chosen, among in ((top1, first, probs), (top2, second, left)):
                then(nc.vector.tensor_reduce(best[:], among[:], AX_X, ALU.max))
                then(nc.vector.tensor_tensor(chosen[:], among[:], spread(best), ALU.is_equal))
                then(nc.vector.tensor_tensor(chosen[:], chosen[:], rank[:], ALU.mult))
                then(nc.vector.tensor_reduce(low[:], chosen[:], AX_X, ALU.max))
                then(nc.vector.tensor_tensor(chosen[:], rank[:], spread(low), ALU.is_equal))
                if chosen is first:
                    then(nc.vector.scalar_tensor_tensor(out=left[:], in0=chosen[:], scalar=-2.0, in1=probs[:],
                                                        op0=ALU.mult, op1=ALU.add))
                    hidden_low(1, 1)
                    hidden(2, 0, bank_up[0])
            then(nc.vector.tensor_tensor(tsum[:], top1[:], top2[:], ALU.add))
            then(nc.vector.reciprocal(tinv[:], tsum[:]))
            then(nc.vector.tensor_tensor(first[:], first[:], second[:], ALU.add))
            then(nc.vector.tensor_tensor(first[:], first[:], probs[:], ALU.mult))
            weights = comb[:, 0:NE, :].rearrange("p e t -> p t e")
            then(nc.vector.tensor_tensor(weights, first[:], spread(tinv), ALU.mult))

            def add_down(w, th, j, first, tiles=range(4)):
                for i in tiles:
                    t = 4 * th + i
                    wait(dve, d_mm, 4 * w + i + 1)
                    if first:
                        nc.vector.tensor_scalar(acc2[:, t, :], bank_down[i], comb_e[:, j, t:t + 1], None,
                                                ALU.mult).then_inc(d_added, 1)
                        continue
                    wait(dve, d_added, 4 * w + i - 7)
                    nc.vector.scalar_tensor_tensor(out=acc2[:, t, :], in0=bank_down[i], scalar=comb_e[:, j, t:t + 1],
                                                   in1=acc2[:, t, :], op0=ALU.mult, op1=ALU.add).then_inc(d_added, 1)

            def y_stats(p):
                dve.wait_ge(d_added, 4 * UNITS - 8 + 2 * p + 2)
                stats(("y", p), acc2)

            def pair_units(i, first, last):
                for j in range(2):
                    for th in range(2):
                        w = 4 * i + 2 * j + th
                        if last and w == UNITS - 1:
                            dve.wait_ge(comb_e_done, NX)
                            add_down(w - 1, 0, 1, False)
                            y_stats(0)
                            y_stats(1)
                            dve.wait_ge(silu_done, UNITS)
                            for half in range(2):
                                at = slice(half * 2 * P, (half + 1) * 2 * P)
                                dve.wait_ge(u_mm, UNITS + half)
                                nc.vector.tensor_tensor(hid[1][:, at], silu[1][:, at], bank_last_up[half][:, at],
                                                        ALU.mult).then_inc(hid_done, 1)
                            for half in range(2):
                                at = slice(half * 2 * P, (half + 1) * 2 * P)
                                dve.wait_ge(hid_hi_done, UNITS + half)
                                nc.vector.tensor_tensor(hid_lo[1][:, at], hid[1][:, at], fp(hid_hi[1][:, at]),
                                                        ALU.subtract).then_inc(hid_lo_done, 1)
                        elif not (first and w == 0):
                            if not (first and w < 3):
                                hidden(w, th, bank_up[th])
                            if not (first and w < 2):
                                hidden_low(w, th)
                        if last and w == UNITS - 1:
                            for p in (2, 3):
                                add_down(w, 1, 1, False, range(2 * p - 4, 2 * p - 2))
                                y_stats(p)
                        elif not (first and j == 0 and th == 0):
                            pj, pth = (j, 0) if th == 1 else (1 - j, 1)
                            if pth == 0:
                                wait(dve, comb_e_done, 2 * i + j + 1)
                            add_down(w - 1, pth, pj, first and w <= 2)
                        if th == 0:
                            nc.vector.tensor_copy(comb_e[:, j, :].rearrange("p (a t) -> p a t", a=1),
                                                  comb[:, bass.ds(2 * i + j, 1), :]).then_inc(comb_e_done, 1)

            pair_units(0, True, False)
            with dve.Fori(1, NX // 2 - 1) as i:
                pair_units(i, False, False)
            pair_units(NX // 2 - 1, False, True)
            for t in range(4, TILES):
                dve.wait_ge(normed, normed_count(("y", t // 2), t % 2))
                nc.vector.tensor_tensor(acc2[:, t, :], acc2[:, t, :], x1[:, t, :], ALU.add).then_inc(y_added_dve, 1)

        @block.scalar
        def _(act):
            def copy(dst, src):
                return nc.scalar.activation(dst, src, ACT.Copy)

            def normalise(what, dst, src):
                act.wait_ge(shift_done, nth[what] + 1)
                for k in range(1 if nth[what] < 2 else 2):
                    t = 2 * what[1] + k
                    nc.scalar.activation(dst[:, t % dst.shape[1], :], src[:, t, :], ACT.Identity,
                                         scale=rstd[:, t:t + 1], bias=shift[:, t:t + 1]).then_inc(normed, 1)

            def turned(i):
                t = i % TILES
                act.wait_ge(turn_mm, i + 1)
                copy(xT_hi[:, :, t * P:(t + 1) * P],
                     bank_turn[i].rearrange("p (c q) -> p c q", c=CH)).then_inc(xT_hi_done, 1)

            def even_latents(j):
                act.wait_ge(lat_mm, j + 1)
                half, hp = j // 4, j % 4
                src = bank_lat[j % 3][0:64, :].rearrange("p (b t c r) -> p r c b t", b=2, t=32, c=4)
                for r in range(2):
                    for i, part in enumerate((lat_k, lat_v)):
                        dst = part[64 * r:64 * r + 64, :, half * PAIR:(half + 1) * PAIR].rearrange(
                            "p c (b t) -> p c b t", b=2)[:, :, :, 2 * hp * 32:2 * hp * 32 + 32]
                        copy(dst, src[:, r, 2 * i:2 * i + 2]).then_inc(lat_even_done, 1)

            def latent_high(c):
                copy(wl_hi[:, c, :], wl_raw[:, c, :]).then_inc(wl_hi_done, 1)

            normalise(("x", 0), x_in, x_in)
            act.wait_ge(wl_landed, 16)
            latent_high(0)
            normalise(("x", 1), x_in, x_in)
            turned(0)
            turned(1)
            turned(2)
            turned(3)
            latent_high(1)
            normalise(("x", 2), x_in, x_in)
            normalise(("x", 3), x_in, x_in)
            def keys_high(half):
                act.wait_ge(lat_even_done, 16 * half + 16)
                act.wait_ge(lat_odd_done, 16 * half + 16)
                cols = slice(half * PAIR, (half + 1) * PAIR)
                copy(lat_k_hi[:, :, cols], lat_k[:, :, cols]).then_inc(lat_k_hi_done, 1)

            for j in range(4):
                even_latents(j)
                turned(4 + j)
            keys_high(0)

            def k_high(count, par):
                wait(act, kv_mm, count)
                copy(k_first[par][:], psKV[:].rearrange("p (b t k) -> p b t k", b=2, t=2)[:, :, 0, :])
                copy(k_hi[par][:], psKV[:]).then_inc(kv_hi_done, 1)

            def v_high(count, par):
                wait(act, kv_mm, count)
                copy(v_hi[par][:].rearrange("p t d -> p (t d)"), psKV[:]).then_inc(kv_hi_done, 1)

            def q_high(count, par, h):
                wait(act, q_mm, count)
                tiles = psQ[:].rearrange("p (b t q) -> p b t q", b=2, t=2)
                copy(q_first[par][:, h], tiles[:, :, 0, :])
                copy(q_hi[par][:, h], tiles[:, :, 1, :]).then_inc(q_hi_done, 1)

            def exponentials(n, l):
                wait(act, nmax_done, n + 1)
                for i in range(4):
                    p = s_sb[l % 2][:, i // 2, QT[i % 2]]
                    nc.scalar.activation(p, p, ACT.Exp, bias=nmax[:, l % 2, i:i + 1],
                                         accum_out=rsum[:, l % 2, i:i + 1]).then_inc(exp_done, 1)

            for h in range(HPG):
                q_high(h + 1, 0, h)
                if h == 1:
                    v_high(2, 0)
                even_latents(4 + h)
                if h == 0:
                    k_high(1, 0)
                if h == 1:
                    exponentials(0, 0)
            keys_high(1)

            def steps(g, first, last):
                for l in range(STEPS):
                    n = STEPS * g + l
                    par, s = l // 4, l % 4
                    wait(act, pT_mm, n + 1)
                    wait(act, o_mm, n)
                    copy(pT_hi[:], psT[:].rearrange("p a b -> p (a b)")[:, 0:768]).then_inc(pT_hi_done, 1)
                    if not (last and l == STEPS - 1):
                        exponentials(n + 1, (l + 1) % STEPS)
                    if not (last and par == 1):
                        q_high(n + 5, 1 - par, s)
                        if s == 0:
                            k_high(4 * g + 2 * par + 3, 1 - par)
                        if s == 1:
                            v_high(4 * g + 2 * par + 4, 1 - par)
                    wait(act, o_mm, n + 1)
                    b_in, hp = s // 2, l % 2
                    if not (first and l < 4):
                        wait(act, w_mm, n - 2 if hp == 0 else n - 3)
                    copy(o_hi[:, b_in, 2 * hp:2 * hp + 2, :],
                         psO[:].rearrange("p (j q) -> p j q", j=2)).then_inc(o_hi_done, 1)
                    if last and l == 4:
                        normalise(("a", 0), acc, acc)
                    if last and l == 5:
                        normalise(("b", 0), xn, x1)
                    if last and l == 6:
                        turned(TILES)
                        turned(TILES + 1)
                        normalise(("a", 1), acc, acc)
                    if last and l == 7:
                        normalise(("b", 1), xn, x1)

            groups(act, steps)

            def by_expert_copy(th):
                act.wait_ge(by_expert_mm, th + 1)
                copy(by_expert[:, th * HALF:(th + 1) * HALF], psO[0:2 * NE, :]).then_inc(by_expert_done, 1)

            def silu_gate(w, th):
                wait(act, g_mm, 3 if isinstance(w, int) and w == 1 else w + 1)
                wait(act, hid_done, w - 1)
                nc.scalar.activation(silu[th][:], bank_gate[th], ACT.Silu).then_inc(silu_done, 1)

            def hidden_high(w, th):
                wait(act, hid_done, w + 1)
                wait(act, d_mm, 4 * w - 4)
                copy(hid_hi[th][:], hid[th][:]).then_inc(hid_hi_done, 1)

            normalise(("a", 2), acc, acc)
            turned(TILES + 2)
            turned(TILES + 3)
            silu_gate(0, 0)
            normalise(("a", 3), acc, acc)
            by_expert_copy(0)
            normalise(("b", 2), xn, x1)
            hidden_high(0, 0)
            turned(TILES + 4)
            turned(TILES + 5)
            normalise(("b", 3), xn, x1)
            turned(TILES + 6)
            turned(TILES + 7)
            by_expert_copy(1)
            silu_gate(1, 1)
            act.wait_ge(router_step, ROUTER_READ)
            nc.scalar.activation(probs[:], probs[:], ACT.Exp).then_inc(router_exp, 1)

            hidden_high(1, 1)
            for w in range(2, 4):
                silu_gate(w, w % 2)
                hidden_high(w, w % 2)
            with act.Fori(1, NX // 2 - 1) as i:
                for w in range(4):
                    silu_gate(4 * i + w, w % 2)
                    hidden_high(4 * i + w, w % 2)
            for w in range(UNITS - 4, UNITS):
                silu_gate(w, w % 2)
                if w < UNITS - 1:
                    hidden_high(w, w % 2)
            act.wait_ge(d_mm, 4 * UNITS - 8)
            for half in range(2):
                at = slice(half * 2 * P, (half + 1) * 2 * P)
                act.wait_ge(hid_done, UNITS + half)
                copy(hid_hi[1][:, at], hid[1][:, at]).then_inc(hid_hi_done, 1)
            for p in range(4):
                normalise(("y", p), acc2, acc2)


def kernel(L0_attn_hidden_states, L0_attn_Wq, L0_attn_Wk_down, L0_attn_Wv_down, L0_attn_Wk_up, L0_attn_Wv_up,
           L0_attn_Wo, L0_ffn_gate_w, L0_ffn_w_gate_up, L0_ffn_w_down, L0_ffn_shared_w_gate_up,
           L0_ffn_shared_w_down):
    import numpy as _np
    import concourse.bacc as _bacc
    from concourse import mybir as _mybir
    from concourse.bass_utils import run_bass_kernel_spmd as _run

    c = _np.ascontiguousarray
    heads = NG * HPG
    w_down_k = _np.asarray(L0_attn_Wk_down).reshape(NG, 32, HID)
    w_down_v = _np.asarray(L0_attn_Wv_down).reshape(NG, 32, HID)
    lat = _np.concatenate([w_down_k, w_down_v], axis=1).reshape(HID, CH, P)
    w_gu = _np.asarray(L0_ffn_w_gate_up).reshape(NE, 2, INTER, HID)
    s_gu = _np.asarray(L0_ffn_shared_w_gate_up).reshape(2, NX - NE, INTER, HID).transpose(1, 0, 2, 3)
    gu = _np.concatenate([w_gu, s_gu], axis=0).reshape(NX, 2 * INTER, CH, P)
    s_dn = _np.asarray(L0_ffn_shared_w_down).reshape(HID, NX - NE, INTER).transpose(1, 2, 0)
    up = _np.stack([_np.asarray(L0_attn_Wk_up), _np.asarray(L0_attn_Wv_up)]).reshape(2, NG, D, 2, P)
    arrays = {
        "x": c(_np.asarray(L0_attn_hidden_states).reshape(T, HID)),
        "w_lat": c(lat.transpose(2, 1, 0).reshape(P, CH * HID)),
        "w_q": c(_np.asarray(L0_attn_Wq).reshape(heads, D, CH, P).transpose(0, 3, 2, 1).reshape(heads, P, CH * D)),
        "w_o": c(_np.asarray(L0_attn_Wo).reshape(HID, heads, D).transpose(1, 2, 0)),
        "w_kv": c(up.transpose(1, 4, 0, 3, 2).reshape(NG, P, 4 * D)),
        "w_gate": c(_np.asarray(L0_ffn_gate_w).reshape(NE, CH, P).transpose(2, 1, 0).reshape(P, CH * NE)),
        "w_gu": c(gu.transpose(0, 3, 2, 1).reshape(NX, P, CH * 2 * INTER)),
        "w_dn": c(_np.concatenate([_np.asarray(L0_ffn_w_down).transpose(0, 2, 1), s_dn], axis=0)),
    }
    nc = _bacc.Bacc("TRN2", target_bir_lowering=False, num_devices=1)
    args = [nc.dram_tensor(n, a.shape, _mybir.dt.from_np(a.dtype), kind="ExternalInput").ap()
            for n, a in arrays.items()]
    args.append(nc.dram_tensor("out", (T, HID), _mybir.dt.float32, kind="ExternalOutput").ap())
    build_program(nc, *args)
    r = _run(nc, [arrays], core_ids=[0])
    return _np.asarray(r.results[0]["out"]).reshape(B, S, HID)
```
